# Optimizing a Trainium2 kernel written in Bass

```python
import numpy as np
import jax
import jax.numpy as jnp

def _softmax(x, axis=-1):
    return jax.nn.softmax(x, axis=axis)

def _gelu(x):
    return jax.nn.gelu(x, approximate=True)

def _silu(x):
    return jax.nn.silu(x)

def _sigmoid(x):
    return jax.nn.sigmoid(x)

def _layernorm(x, axis=-1, eps=1e-05):
    m = jnp.mean(x, axis=axis, keepdims=True)
    v = jnp.var(x, axis=axis, keepdims=True)
    return (x - m) / jnp.sqrt(v + eps)

def _scatter_add(tgt, idx, src, axis=0):
    return tgt.at[idx].add(src)

def _segment_sum(src, seg, n):
    return jax.ops.segment_sum(src, seg, n)
kernel_name = 'mk_prb_d1_jaxref_r4_a898a2'

def setup_inputs(seed: int=0):
    np.random.seed(seed)
    _w = jnp.asarray

    def _L0_attn_setup():
        import jax, jax.numpy as jnp
        import numpy as np
        B, S, D = (2, 512, 1024)
        H = 32
        HD = D // H
        THETA = 10000.0

        def _rope_cos_sin(seq_len, head_dim, theta=THETA):
            inv = 1.0 / theta ** (np.arange(0, head_dim, 2)[:head_dim // 2].astype(np.float32) / head_dim)
            t = np.arange(seq_len)
            f = np.outer(t, inv).astype(np.float32)
            return (jnp.asarray(np.cos(f)), jnp.asarray(np.sin(f)))

        def _apply_rotary(x, cos, sin):
            xr = x.astype(jnp.float32).reshape(*x.shape[:-1], HD // 2, 2)
            x0, x1 = (xr[..., 0], xr[..., 1])
            c = cos[None, :, None, :]
            s = sin[None, :, None, :]
            o0 = x0 * c - x1 * s
            o1 = x0 * s + x1 * c
            return jnp.stack((o0, o1), axis=-1).reshape(*x.shape[:-1], HD)
        key = jax.random.key(seed)
        ks = jax.random.split(key, 5)
        std = 0.02
        return {'x': jax.random.normal(ks[0], (B, S, D), dtype=jnp.float32), 'wq': jax.random.normal(ks[1], (D, D), dtype=jnp.float32) * std, 'wk': jax.random.normal(ks[2], (D, D), dtype=jnp.float32) * std, 'wv': jax.random.normal(ks[3], (D, D), dtype=jnp.float32) * std, 'wo': jax.random.normal(ks[4], (D, D), dtype=jnp.float32) * std}
    _L0_attn_in = _L0_attn_setup()

    def _L0_ffn_setup():
        import jax, jax.numpy as jnp
        import numpy as np
        OUT_F = 1024
        IN_F = 1024
        GROUP = 64

        def _dequantize(W_q, scale, zero):
            low = (W_q & 15).astype(jnp.float32)
            high = (W_q >> 4).astype(jnp.float32)
            unpacked = jnp.stack([low, high], axis=-1).reshape(-1)
            grouped = unpacked.reshape(-1, GROUP)
            w = (grouped - zero[:, None]) * scale[:, None]
            return w.reshape(OUT_F, IN_F)
        key = jax.random.key(seed)
        k1, k2, k3, k4 = jax.random.split(key, 4)
        n_packed = OUT_F * IN_F // 2
        n_groups = OUT_F * IN_F // GROUP
        x = jax.random.normal(k1, (4, 512, IN_F), dtype=jnp.float32)
        W_q = jax.random.randint(k2, (n_packed,), 0, 64, dtype=jnp.int32)
        scale = jax.random.uniform(k3, (n_groups,), dtype=jnp.float32) * 0.01 + 0.0001
        zero = jax.random.uniform(k4, (n_groups,), dtype=jnp.float32) * 8.0
        return {'x': x, 'W_q': W_q, 'scale': scale, 'zero': zero}
    _L0_ffn_in = _L0_ffn_setup()
    _d = {'L0_attn_x': _L0_attn_in['x'], 'L0_attn_wq': _L0_attn_in['wq'], 'L0_attn_wk': _L0_attn_in['wk'], 'L0_attn_wv': _L0_attn_in['wv'], 'L0_attn_wo': _L0_attn_in['wo'], 'L0_ffn_W_q': _L0_ffn_in['W_q'], 'L0_ffn_scale': _L0_ffn_in['scale'], 'L0_ffn_zero': _L0_ffn_in['zero']}
    _x0 = _d['L0_attn_x']
    _d['L0_attn_x'] = jax.random.normal(jax.random.fold_in(jax.random.key(seed), 1), (2, 1024, 1024), dtype=_x0.dtype)
    del _x0
    return _d

def reference(L0_attn_x, L0_attn_wq, L0_attn_wk, L0_attn_wv, L0_attn_wo, L0_ffn_W_q, L0_ffn_scale, L0_ffn_zero):

    def _L0_attn_ref(x, wq, wk, wv, wo):
        import jax, jax.numpy as jnp
        import numpy as np
        B, S, D = (2, 512, 1024)
        H = 32
        HD = D // H
        THETA = 10000.0

        def _rope_cos_sin(seq_len, head_dim, theta=THETA):
            inv = 1.0 / theta ** (np.arange(0, head_dim, 2)[:head_dim // 2].astype(np.float32) / head_dim)
            t = np.arange(seq_len)
            f = np.outer(t, inv).astype(np.float32)
            return (jnp.asarray(np.cos(f)), jnp.asarray(np.sin(f)))

        def _apply_rotary(x, cos, sin):
            xr = x.astype(jnp.float32).reshape(*x.shape[:-1], HD // 2, 2)
            x0, x1 = (xr[..., 0], xr[..., 1])
            c = cos[None, :, None, :]
            s = sin[None, :, None, :]
            o0 = x0 * c - x1 * s
            o1 = x0 * s + x1 * c
            return jnp.stack((o0, o1), axis=-1).reshape(*x.shape[:-1], HD)
        b, s, d = x.shape
        q = (x @ wq).reshape(b, s, H, HD)
        k = (x @ wk).reshape(b, s, H, HD)
        v = (x @ wv).reshape(b, s, H, HD)
        cos, sin = _rope_cos_sin(s, HD)
        q = _apply_rotary(q, cos, sin)
        k = _apply_rotary(k, cos, sin)
        scale = 1.0 / jnp.sqrt(jnp.float32(HD))
        scores = jnp.einsum('bqhd,bkhd->bhqk', q, k) * scale
        causal = jnp.tril(jnp.ones((s, s), dtype=bool))
        scores = jnp.where(causal[None, None], scores, jnp.finfo(scores.dtype).min)
        probs = jax.nn.softmax(scores, axis=-1)
        out = jnp.einsum('bhqk,bkhd->bqhd', probs, v).reshape(b, s, d)
        return out @ wo

    def _L0_ffn_ref(x, W_q, scale, zero):
        import jax, jax.numpy as jnp
        import numpy as np
        OUT_F = 1024
        IN_F = 1024
        GROUP = 64

        def _dequantize(W_q, scale, zero):
            low = (W_q & 15).astype(jnp.float32)
            high = (W_q >> 4).astype(jnp.float32)
            unpacked = jnp.stack([low, high], axis=-1).reshape(-1)
            grouped = unpacked.reshape(-1, GROUP)
            w = (grouped - zero[:, None]) * scale[:, None]
            return w.reshape(OUT_F, IN_F)
        w = _dequantize(W_q, scale, zero)
        return jnp.einsum('bsi,oi->bso', x, w)
    x = L0_attn_x
    xn = _layernorm(x, axis=-1)
    x = x + _L0_attn_ref(xn, L0_attn_wq, L0_attn_wk, L0_attn_wv, L0_attn_wo) + _L0_ffn_ref(xn, L0_ffn_W_q, L0_ffn_scale, L0_ffn_zero)
    return x

_drawn_inputs = setup_inputs


def setup_inputs(seed=0):
    import zlib

    import numpy as np

    out = dict(_drawn_inputs(seed))
    spreads = {}
    factors = {'L0_attn_wq': 5.811, 'L0_attn_wk': 5.783}
    for name, (base, spread) in spreads.items():
        noise = np.random.default_rng([zlib.crc32(name.encode()), seed]).standard_normal(out[name].shape)
        drawn = base * np.exp(spread * noise) if base else spread * noise
        out[name] = jnp.asarray(drawn.astype(out[name].dtype))
    for name, factor in factors.items():
        out[name] = (out[name] * factor).astype(out[name].dtype)
    return out
```

```python
from contextlib import ExitStack

import concourse.bass as bass
from concourse import mybir

F32 = mybir.dt.float32
F16 = mybir.dt.float16
I32 = mybir.dt.int32
ALU = mybir.AluOpType
ACT = mybir.ActivationFunctionType
AX = mybir.AxisListType
RMAX = bass.bass_isa.ReduceOp.max

P = 128
B, S, D = 2, 1024, 1024
H, HD = 32, 32
TOK = B * S
IC = D // P
TT = TOK // P
QT = S // P
PAIRS = B * H
GROUP = 64
NG = D // GROUP
VW = 2 * HD + 1
EPS = 1e-5

XN_SCALE = 2.0 ** 10
W_TOP = 2.0 ** 14
QK_SCALE = 2.0 ** -23
V_SCALE = 2.0 ** -20
MAX_SCALE = 2.0 ** -15
MASKED = 2.0 ** 60

KEY_ORDER = [0, 1, 7, 2, 6, 3, 5, 4]
BLOCKS = [(j, t) for j in KEY_ORDER for t in range(j, QT)]
SLOT = {jt: n for n, jt in enumerate(BLOCKS)}
UNIT = 4
UNITS = len(BLOCKS) // UNIT
CHUNK = 3
CHUNKS = UNITS // CHUNK
CW = CHUNK * UNIT * P
DIAGONALS = [[(0, 8, 2)], [(15, 1, 1), (16, 6, 2)], [(24, 8, 2), (29, 1, 1)]]
SEGMENTS = [(t, 0, 512, False) for t in range(4, QT)] + \
           [(t, 0, (t + 1) * P, True) for t in range(4)] + \
           [(t, 512, (t - 3) * P, True) for t in range(4, QT)]
NSEG = len(SEGMENTS)


def unit_runs(u):
    runs = []
    for k in range(UNIT):
        j, t = BLOCKS[u * UNIT + k]
        if runs and runs[-1][1] == j:
            runs[-1][3] += 1
        else:
            runs.append([k * P, j, t, 1])
    return runs


def wait(eng, sem, value):
    if isinstance(value, int) and value <= 0:
        return
    eng.wait_ge(sem, value)


def held(eng, value):
    return value if isinstance(value, int) else eng.snap(value)


def build(nc, x, wq, wk, wv, wo, w_packed, w_scale, w_zero, cos_t, sin_t, out):
    q_scr = nc.dram_tensor("q_scr", (B, H, 2, HD, S), F16, kind="Internal").ap()
    k_scr = nc.dram_tensor("k_scr", (B, H, 2, HD, S), F16, kind="Internal").ap()
    v_scr = nc.dram_tensor("v_scr", (B, H, 2, P, 4 * VW), F16, kind="Internal").ap()
    y_scr = nc.dram_tensor("y_scr", (TT, P, D), F32, kind="Internal").ap()
    o_scr = nc.dram_tensor("o_scr", (B * IC, P, 2, S), F16, kind="Internal").ap()
    x_tiles = x.rearrange("b (t p) d -> (b t) p d", p=P)
    out_tiles = out.rearrange("b (t p) d -> (b t) p d", p=P)

    with ExitStack() as whole:
        def sb(ctx, name, shape, dt):
            return ctx.enter_context(nc.sbuf_tensor(name, shape, dt))

        def sem(name):
            return whole.enter_context(nc.semaphore(name))

        banks = [whole.enter_context(nc.psum_tensor(f"bank{i}", [P, 512], F32)) for i in range(8)]
        ident = sb(whole, "ident", [P, P], F16)
        w_absmax = sb(whole, "w_absmax", [P, 5], F32)
        w_pow2 = sb(whole, "w_pow2", [P, 5], F32)
        w_up = sb(whole, "w_up", [P, 5], F32)
        w_down = sb(whole, "w_down", [P, 5], F32)
        exp_scale = sb(whole, "exp_scale", [P, 1], F32)
        attn_scale = sb(whole, "attn_scale", [P, 1], F32)
        ffn_scale = sb(whole, "ffn_scale", [P, 1], F32)
        xnT_h = sb(whole, "xnT_h", [P, IC, TOK], F16)
        xnT_l = sb(whole, "xnT_l", [P, IC, TOK], F16)

        def pow2_scales(dve, chain, c0, c1):
            cs = slice(c0, c1)
            chain(nc.vector.tensor_scalar(w_pow2[:, cs], w_absmax[:, cs], 1e-30, None, ALU.max))
            chain(nc.vector.tensor_scalar(w_pow2[:, cs].bitcast(I32), w_pow2[:, cs].bitcast(I32),
                                          0x7F800000, None, ALU.bitwise_and))
            chain(nc.vector.reciprocal(w_up[:, cs], w_pow2[:, cs]))
            chain(nc.vector.tensor_scalar(w_up[:, cs], w_up[:, cs], W_TOP, None, ALU.mult))
            chain(nc.vector.tensor_scalar(w_down[:, cs], w_pow2[:, cs], 1.0 / W_TOP, None, ALU.mult))

        step1 = ExitStack()
        with step1:
            GT = 4
            w_raw = sb(step1, "w_raw", [P, IC, D], F32)
            wv_h = sb(step1, "wv_h", [P, IC, D], F16)
            wv_l = sb(step1, "wv_l", [P, IC, D], F16)
            xt = sb(step1, "xt", [P, 2, GT, D], F32)
            xh = sb(step1, "xh", [P, 2, D], F16)
            xl = sb(step1, "xl", [P, 2, D], F16)
            stats = sb(step1, "stats", [P, GT, 2, 6], F32)
            mv = sb(step1, "mv", [P, GT, 2], F32)
            sd = sb(step1, "sd", [P, GT], F32)
            ve = sb(step1, "ve", [P, GT], F32)
            rstd = sb(step1, "rstd", [P, GT], F32)
            tmp = sb(step1, "tmp", [P, GT], F32)
            shift = sb(step1, "shift", [P, GT], F32)
            v_st = sb(step1, "v_st", [P, 2, H, GT * VW], F16)
            wmx = sb(step1, "wmx", [P, 16], F32)

            s_id = sem("ident_ready")
            s_wv = [sem(f"wv_loaded{c}") for c in range(4)]
            s_bg = [sem(f"weight_loaded{c}") for c in range(4)]
            s_x = [sem(f"x_loaded{k}") for k in range(2)]
            s_chain = sem("dve_small_done")
            s_wmax = sem("wv_max_ready")
            s_wall = sem("wv_max_all_ready")
            s_wup = sem("wv_scale_ready")
            s_wh = sem("wv_high_ready")
            s_wl = sem("wv_low_ready")
            s_var = sem("variance_ready")
            s_sd = sem("deviation_ready")
            s_rs = sem("rstd_ready")
            s_xn = sem("xn_ready")
            s_xh = sem("xn_high_ready")
            s_xl = sem("xn_low_ready")
            s_tr = sem("xn_transposed")
            s_th = sem("xnT_high_stored")
            s_tl = sem("xnT_low_stored")
            s_v = sem("v_product_ready")
            s_vh = sem("v_high_ready")
            s_vl = sem("v_low_ready")
            s_vw = [sem(f"v_written{k}") for k in range(2)]
            s_bgm = sem("weight_slab_reduced")
            s_all4 = sem("weight_max_all_ready")
            NT1 = TT // GT
            slabs = [(w, c) for w in (wq, wk, wo) for c in range(4)]
            slab_view = [w.rearrange("(c p) n -> p c n", p=P)[:, 2 * c:2 * c + 2, :] for w, c in slabs]

            with nc.Block("norm_v") as block:
                @block.sync
                def _(sp):
                    wv_view = wv.rearrange("(c p) n -> p c n", p=P)
                    for c in range(4):
                        sp.dma_start(w_raw[:, 2 * c:2 * c + 2, :], wv_view[:, 2 * c:2 * c + 2, :]).then_inc(s_wv[c], 16)
                    for k in range(2):
                        sp.dma_start(xt[:, k], x_tiles[GT * k:GT * k + GT].rearrange("t p d -> p t d")).then_inc(s_x[k], 16)
                    wait(sp, s_wh, IC)
                    wait(sp, s_wl, IC)
                    for n in range(12):
                        if n >= 4:
                            wait(sp, s_bgm, n - 3)
                        sp.dma_start(w_raw[:, 2 * (n % 4):2 * (n % 4) + 2, :], slab_view[n]).then_inc(s_bg[n % 4], 16)
                        if n % 6 == 5:
                            k = n // 6
                            wait(sp, s_xl, GT * (k + 1))
                            sp.dma_start(xt[:, k], x_tiles[GT * (k + 2):GT * (k + 3)].rearrange("t p d -> p t d")).then_inc(s_x[k], 16)

                @block.gpsimd
                def _(pool):
                    pool.memset(ident[:], 0.0).then_inc(s_id, 1)
                    pool.wait_ge(s_id, 1)
                    pool.affine_select(out=ident[:], in_=ident[:], compare_op=ALU.not_equal, fill=1.0, base=0,
                                       pattern=[[-1, P]], channel_multiplier=1).then_inc(s_id, 1)
                    for k in range(2):
                        for h in range(GT):
                            pool.memset(v_st[:, k, :, (h + 1) * VW - 1:(h + 1) * VW], 1.0).then_inc(s_id, 1)
                    pool.wait_ge(s_wmax, 1)
                    pool.partition_all_reduce(w_absmax[:, 2:3], wmx[:, 4:5], P, RMAX).then_inc(s_wall, 1)
                    for it in range(NT1):
                        wait(pool, s_vh, 8 * (it + 1))
                        wait(pool, s_vl, 8 * (it + 1))
                        if it == 0:
                            pool.wait_ge(s_id, 2 + 2 * GT)
                        pool.dma_start(v_scr[it // 2, :, it % 2].rearrange("h p c -> p h c"), v_st[:, it % 2]).then_inc(s_vw[it % 2], 16)
                    pool.wait_ge(s_bgm, 13)
                    pool.partition_all_reduce(wmx[:, 13:16], wmx[:, 13:16], P, RMAX).then_inc(s_all4, 1)
                    for k in range(2):
                        wait(pool, s_vw[k], 32)

                @block.scalar
                def _(act):
                    act.wait_ge(s_wup, 1)
                    for c in range(IC):
                        act.activation(wv_h[:, c, :], w_raw[:, c, :], ACT.Copy, scale=w_up[:, 2:3]).then_inc(s_wh, 1)

                    def v_high(t):
                        for n in range(2):
                            wait(act, s_v, 2 * t + n + 1)
                            k, r = (t // GT) % 2, t % GT
                            if t >= 2 * GT and n == 0 and r == 0:
                                wait(act, s_vw[k], 16)
                            act.activation(v_st[:, k, 16 * n:16 * n + 16, r * VW:r * VW + HD],
                                           banks[4 + 2 * (t % 2) + n][:].rearrange("p (h d) -> p h d", d=HD),
                                           ACT.Copy, scale=V_SCALE).then_inc(s_vh, 1)

                    for it in range(NT1):
                        act.wait_ge(s_var, it + 1)
                        act.activation(sd[:], ve[:], ACT.Sqrt).then_inc(s_sd, 1)
                        act.wait_ge(s_rs, it + 1)
                        for r in range(GT):
                            t = it * GT + r
                            wait(act, s_tr, 2 * (t - 1))
                            act.activation(xh[:, t % 2], xt[:, it % 2, r], ACT.Identity, bias=shift[:, r:r + 1],
                                           scale=rstd[:, r:r + 1]).then_inc(s_xh, 1)
                            act.wait_ge(s_tr, 2 * t + 1)
                            act.activation(xnT_h[:, :, t * P:(t + 1) * P],
                                           banks[0 + 2 * (t % 2)][:].bitcast(F16).rearrange("p (c s) -> p c s", s=P),
                                           ACT.Copy).then_inc(s_th, 1)
                            if t >= 1:
                                v_high(t - 1)
                    v_high(TT - 1)

                @block.vector
                def _(dve):
                    done = [0]

                    def chain(ins):
                        done[0] += 1
                        ins.then_inc(s_chain, 1)
                        dve.wait_ge(s_chain, done[0])

                    for c in range(4):
                        dve.wait_ge(s_wv[c], 16)
                        chain(nc.vector.tensor_reduce(wmx[:, c:c + 1], w_raw[:, 2 * c:2 * c + 2, :], AX.XY, ALU.max,
                                                      apply_absolute_value=True))
                    nc.vector.tensor_reduce(wmx[:, 4:5], wmx[:, 0:4], AX.X, ALU.max).then_inc(s_wmax, 1)

                    def split_wv():
                        dve.wait_ge(s_wall, 1)
                        pow2_scales(dve, chain, 2, 3)
                        chain(nc.vector.tensor_copy(tmp[:, 0:1], w_up[:, 2:3]))
                        nc.vector.tensor_copy(tmp[:, 1:2], w_up[:, 2:3]).then_inc(s_wup, 1)
                        for c in range(IC):
                            dve.wait_ge(s_wh, c + 1)
                            nc.vector.scalar_tensor_tensor(wv_l[:, c, :], w_raw[:, c, :], w_up[:, 2:3], wv_h[:, c, :],
                                                           ALU.mult, ALU.subtract).then_inc(s_wl, 1)

                    def v_low(t):
                        for n in range(2):
                            dve.wait_ge(s_vh, 2 * t + n + 1)
                            k, r = (t // GT) % 2, t % GT
                            nc.vector.scalar_tensor_tensor(
                                v_st[:, k, 16 * n:16 * n + 16, r * VW + HD:r * VW + 2 * HD],
                                banks[4 + 2 * (t % 2) + n][:].rearrange("p (h d) -> p h d", d=HD), V_SCALE,
                                v_st[:, k, 16 * n:16 * n + 16, r * VW:r * VW + HD],
                                ALU.mult, ALU.subtract).then_inc(s_vl, 1)

                    slab = [0]

                    def slab_max():
                        n = slab[0]
                        if n < 12:
                            slab[0] += 1
                            dve.wait_ge(s_bg[n % 4], 16 * (n // 4 + 1))
                            nc.vector.tensor_reduce(wmx[:, n:n + 1], w_raw[:, 2 * (n % 4):2 * (n % 4) + 2, :], AX.XY,
                                                    ALU.max, apply_absolute_value=True).then_inc(s_bgm, 1)

                    for it in range(NT1):
                        dve.wait_ge(s_x[it % 2], 16 * (it // 2 + 1))
                        for r in range(GT):
                            for k in range(2):
                                ins = nc.vector.bn_stats(stats[:, r, k, :], xt[:, it % 2, r, 512 * k:512 * k + 512])
                        chain(ins)
                        for r in range(GT):
                            ins = nc.vector.bn_aggr(mv[:, r, :], stats[:, r, :, :].rearrange("p a b -> p (a b)"))
                        chain(ins)
                        if it == 0:
                            split_wv()
                        nc.vector.tensor_scalar(ve[:], mv[:, :, 1], EPS, None, ALU.add).then_inc(s_var, 1)
                        dve.wait_ge(s_var, it + 1)
                        dve.wait_ge(s_sd, it + 1)
                        chain(nc.vector.reciprocal(rstd[:], sd[:]))
                        chain(nc.vector.tensor_tensor(tmp[:], ve[:], rstd[:], ALU.mult))
                        chain(nc.vector.tensor_tensor(tmp[:], tmp[:], rstd[:], ALU.mult))
                        chain(nc.vector.tensor_scalar(tmp[:], tmp[:], -0.5, 1.5, ALU.mult, ALU.add))
                        chain(nc.vector.tensor_scalar(tmp[:], tmp[:], XN_SCALE, None, ALU.mult))
                        chain(nc.vector.tensor_tensor(rstd[:], rstd[:], tmp[:], ALU.mult))
                        chain(nc.vector.tensor_tensor(tmp[:], mv[:, :, 0], rstd[:], ALU.mult))
                        nc.vector.tensor_scalar(shift[:], tmp[:], -1.0, None, ALU.mult).then_inc(s_rs, 1)
                        dve.wait_ge(s_rs, it + 1)
                        for r in range(GT):
                            t = it * GT + r
                            dve.wait_ge(s_xh, t + 1)
                            chain(nc.vector.tensor_scalar(xt[:, it % 2, r], xt[:, it % 2, r], rstd[:, r:r + 1],
                                                          shift[:, r:r + 1], ALU.mult, ALU.add))
                            wait(dve, s_tr, 2 * (t - 1))
                            nc.vector.tensor_tensor(xl[:, t % 2], xt[:, it % 2, r], xh[:, t % 2],
                                                    ALU.subtract).then_inc(s_xl, 1)
                            dve.wait_ge(s_tr, 2 * t + 2)
                            nc.vector.tensor_copy(xnT_l[:, :, t * P:(t + 1) * P],
                                                  banks[1 + 2 * (t % 2)][:].bitcast(F16).rearrange("p (c s) -> p c s", s=P)
                                                  ).then_inc(s_tl, 1)
                            if t >= 1:
                                v_low(t - 1)
                            slab_max()
                    v_low(TT - 1)
                    dve.wait_ge(s_bgm, 12)
                    for w in range(3):
                        ins = nc.vector.tensor_reduce(wmx[:, 13 + w:14 + w], wmx[:, 4 * w:4 * w + 4], AX.X, ALU.max)
                    ins.then_inc(s_bgm, 1)
                    dve.wait_ge(s_all4, 1)
                    for src, dst in ((13, 0), (14, 1), (15, 3)):
                        chain(nc.vector.tensor_copy(w_absmax[:, dst:dst + 1], wmx[:, src:src + 1]))
                    pow2_scales(dve, chain, 0, 2)
                    pow2_scales(dve, chain, 3, 4)
                    chain(nc.vector.tensor_tensor(exp_scale[:], w_down[:, 0:1], w_down[:, 1:2], ALU.mult))
                    chain(nc.vector.tensor_scalar(exp_scale[:], exp_scale[:], 1.0 / (QK_SCALE * XN_SCALE) ** 2,
                                                  float(HD) ** -0.5, ALU.mult, ALU.mult))
                    chain(nc.vector.tensor_tensor(attn_scale[:], w_down[:, 2:3], w_down[:, 3:4], ALU.mult))
                    chain(nc.vector.tensor_scalar(attn_scale[:], attn_scale[:], 1.0 / (V_SCALE * XN_SCALE), None, ALU.mult))

                @block.tensor
                def _(pe):
                    pe.wait_ge(s_id, 2)

                    def v_product(t):
                        if t == 0:
                            pe.wait_ge(s_wh, IC)
                            pe.wait_ge(s_wl, IC)
                        pe.wait_ge(s_th, t + 1)
                        pe.wait_ge(s_tl, t + 1)
                        for n in range(2):
                            wait(pe, s_vl, 2 * (t - 2) + n + 1)
                            acc = banks[4 + 2 * (t % 2) + n]
                            cols = slice(512 * n, 512 * n + 512)
                            for c in range(IC):
                                hi, lo = xnT_h[:, c, t * P:(t + 1) * P], xnT_l[:, c, t * P:(t + 1) * P]
                                pe.matmul(acc[:], hi, wv_h[:, c, cols], start=(c == 0), stop=False)
                                pe.matmul(acc[:], hi, wv_l[:, c, cols], start=False, stop=False)
                                ins = pe.matmul(acc[:], lo, wv_h[:, c, cols], start=False, stop=(c == IC - 1))
                            ins.then_inc(s_v, 1)

                    for t in range(TT):
                        for part, ready, read, bank in ((xh, s_xh, s_th, 0), (xl, s_xl, s_tl, 1)):
                            pe.wait_ge(ready, t + 1)
                            wait(pe, read, t - 1)
                            dst = banks[bank + 2 * (t % 2)][:].bitcast(F16)
                            for c in range(IC):
                                ins = pe.transpose(dst[:, c * P:(c + 1) * P], part[:, t % 2, c * P:(c + 1) * P], ident[:])
                            ins.then_inc(s_tr, 1)
                        if t >= 1:
                            v_product(t - 1)
                    v_product(TT - 1)

        step2 = ExitStack()
        with step2:
            HG = 8
            NGRP = H // HG
            raw = sb(step2, "qk_raw", [P, 2, IC, 256], F32)
            wh = sb(step2, "qk_wh", [P, 2, IC, 2, P], F16)
            wl = sb(step2, "qk_wl", [P, 2, IC, 2, P], F16)
            cosb = sb(step2, "cosb", [P, S], F32)
            sinb = sb(step2, "sinb", [P, S], F32)
            prod = sb(step2, "prod", [P, 2, 4, 512], F32)
            rot = sb(step2, "rot", [P, 2, 2, 512], F32)
            rh = sb(step2, "rh", [P, 2, 2, 512], F16)
            rl = sb(step2, "rl", [P, 2, 2, 512], F16)
            s_tab = sem("tables_loaded")
            s_raw = [sem(f"qk_weight_loaded{k}") for k in range(2)]
            s_qwh = sem("qk_weight_high")
            s_qwl = sem("qk_weight_low")
            s_ps = sem("qk_product_ready")
            s_pr = sem("rotation_products_ready")
            s_rot = sem("rotated_ready")
            s_rh = sem("rotated_high_ready")
            s_rl = sem("rotated_low_ready")
            s_st = [sem(f"qk_written{k}") for k in range(2)]
            TC = TOK // 512
            CH = 2 * TC

            with nc.Block("qk") as block:
                @block.sync
                def _(sp):
                    sp.dma_start(cosb[:], cos_t).then_inc(s_tab, 16)
                    sp.dma_start(sinb[:], sin_t).then_inc(s_tab, 16)
                    views = [w.rearrange("(c p) n -> p c n", p=P) for w in (wq, wk)]

                    def load(g):
                        for w in range(2):
                            if not isinstance(g, int) or g > 0:
                                wait(sp, s_qwl, 2 * (g - 1) + w + 1)
                            sp.dma_start(raw[:, w], views[w][:, :, bass.ds(g * 256, 256)]).then_inc(s_raw[w], 16)

                    load(0)
                    with sp.Fori(1, NGRP) as g:
                        load(g)

                def chunk_out(eng, g, w, tc, part, ab, src):
                    scr = q_scr if w == 0 else k_scr
                    dst = scr[tc // 2, :, part, 16 * ab:16 * ab + 16, 512 * (tc % 2):512 * (tc % 2) + 512]
                    return eng.dma_start(dst[bass.ds(g * HG, HG)].rearrange("h i s -> h i s"), src)

                @block.gpsimd
                def _(pool):
                    def group(g):
                        for w in range(2):
                            for tc in range(TC):
                                m = w * TC + tc
                                k = m % 2
                                n = g * CH + m
                                wait(pool, s_pr, n + 1)
                                if m >= 2 or not isinstance(g, int):
                                    wait(pool, s_rl, 2 * (n - 1))
                                nc.gpsimd.tensor_tensor(rot[:, k, 0], prod[:, k, 0], prod[:, k, 1], ALU.subtract).then_inc(s_rot, 1)
                                nc.gpsimd.tensor_tensor(rot[:, k, 1], prod[:, k, 2], prod[:, k, 3], ALU.add).then_inc(s_rot, 1)
                    group(0)
                    with pool.Fori(1, NGRP) as g:
                        group(g)

                @block.scalar
                def _(act):
                    def group(g):
                        first = isinstance(g, int)
                        for w in range(2):
                            wait(act, s_raw[w], 16 * (g + 1))
                            if not first:
                                wait(act, s_ps, (g - 1) * CH + (w + 1) * TC)
                            for ab in range(2):
                                act.activation(wh[:, w, :, ab, :], raw[:, w].rearrange("p c (m a) -> p a c m", a=2)[:, ab],
                                               ACT.Copy, scale=w_up[:, w:w + 1]).then_inc(s_qwh, 1)
                        for w in range(2):
                            for tc in range(TC):
                                m = w * TC + tc
                                k = m % 2
                                n = g * CH + m
                                for ab in range(2):
                                    wait(act, s_rot, 2 * n + ab + 1)
                                    if ab == 0 and (m >= 2 or not first):
                                        wait(act, s_st[k], 64 * (g * (CH // 2) + m // 2))
                                    act.activation(rh[:, k, ab], rot[:, k, ab], ACT.Copy).then_inc(s_rh, 1)
                                wait(act, s_rl, 2 * (n + 1))
                                wait(act, s_rh, 2 * (n + 1))
                                for part, src in ((0, rh), (1, rl)):
                                    for ab in range(2):
                                        chunk_out(act, g, w, tc, part, ab, src[:, k, ab]).then_inc(s_st[k], 16)
                    group(0)
                    with act.Fori(1, NGRP) as g:
                        group(g)
                    for k in range(2):
                        act.wait_ge(s_st[k], 64 * NGRP * CH // 2)

                @block.vector
                def _(dve):
                    def group(g):
                        first = isinstance(g, int)
                        if first:
                            dve.wait_ge(s_tab, 32)
                        for w in range(2):
                            for ab in range(2):
                                wait(dve, s_qwh, 4 * g + 2 * w + ab + 1)
                                for c4 in range(2):
                                    cs = slice(4 * c4, 4 * c4 + 4)
                                    ins = nc.vector.scalar_tensor_tensor(
                                        wl[:, w, cs, ab, :], raw[:, w, cs].rearrange("p c (m a) -> p a c m", a=2)[:, ab],
                                        w_up[:, w:w + 1], wh[:, w, cs, ab, :], ALU.mult, ALU.subtract)
                            ins.then_inc(s_qwl, 1)

                        def rotate(m):
                            k = m % 2
                            n = g * CH + m
                            wait(dve, s_ps, n + 1)
                            if m >= 2 or not first:
                                wait(dve, s_rot, 2 * (n - 1))
                            s0 = 512 * (m % 2)
                            c, s = cosb[:, s0:s0 + 512], sinb[:, s0:s0 + 512]
                            even, odd = banks[2 * k][:], banks[2 * k + 1][:]
                            nc.vector.tensor_tensor(prod[:, k, 0], even, c, ALU.mult)
                            nc.vector.tensor_tensor(prod[:, k, 1], odd, s, ALU.mult)
                            nc.vector.tensor_tensor(prod[:, k, 2], even, s, ALU.mult)
                            nc.vector.tensor_tensor(prod[:, k, 3], odd, c, ALU.mult).then_inc(s_pr, 1)

                        def low(m):
                            k = m % 2
                            n = g * CH + m
                            for ab in range(2):
                                wait(dve, s_rh, 2 * n + ab + 1)
                                nc.vector.tensor_tensor(rl[:, k, ab], rot[:, k, ab], rh[:, k, ab],
                                                        ALU.subtract).then_inc(s_rl, 1)

                        for m in range(CH):
                            rotate(m)
                            if m >= 1:
                                low(m - 1)
                        low(CH - 1)
                    group(0)
                    with dve.Fori(1, NGRP) as g:
                        group(g)

                @block.tensor
                def _(pe):
                    def group(g):
                        first = isinstance(g, int)
                        for w in range(2):
                            wait(pe, s_qwh, 4 * g + 2 * w + 2)
                            wait(pe, s_qwl, 2 * g + w + 1)
                            for tc in range(TC):
                                m = w * TC + tc
                                k = m % 2
                                n = g * CH + m
                                if m >= 2 or not first:
                                    wait(pe, s_pr, n - 1)
                                for ab in range(2):
                                    acc = banks[2 * k + ab]
                                    for c in range(IC):
                                        hi = xnT_h[:, c, 512 * tc:512 * tc + 512]
                                        lo = xnT_l[:, c, 512 * tc:512 * tc + 512]
                                        pe.matmul(acc[:], wh[:, w, c, ab], hi, start=(c == 0), stop=False)
                                        pe.matmul(acc[:], wh[:, w, c, ab], lo, start=False, stop=False)
                                        ins = pe.matmul(acc[:], wl[:, w, c, ab], hi, start=False, stop=(c == IC - 1))
                                ins.then_inc(s_ps, 1)
                    group(0)
                    with pe.Fori(1, NGRP) as g:
                        group(g)

        step3_to_5(nc, whole, sb, sem, banks, ident, xnT_h, xnT_l, w_absmax, w_up, w_down, pow2_scales,
                   exp_scale, attn_scale, ffn_scale, q_scr, k_scr, v_scr, y_scr, o_scr, x_tiles, out_tiles,
                   wo, w_packed, w_scale, w_zero)


def step3_to_5(nc, whole, sb, sem, banks, ident, xnT_h, xnT_l, w_absmax, w_up, w_down, pow2_scales,
               exp_scale, attn_scale, ffn_scale, q_scr, k_scr, v_scr, y_scr, o_scr, x_tiles, out_tiles,
               wo, w_packed, w_scale, w_zero):
    wfT_h = sb(whole, "wfT_h", [P, IC, D], F16)
    wfT_l = sb(whole, "wfT_l", [P, IC, D], F16)

    step3 = ExitStack()
    with step3:
        OT = D // P
        packed = sb(step3, "packed", [P, 2, D // 2], I32)
        nib = sb(step3, "nib", [P, 2, 2, D // 2], I32)
        zs = sb(step3, "zs", [P, 2, OT, NG], F32)
        wf = sb(step3, "wf", [P, OT, D], F32)
        wf_h = sb(step3, "wf_h", [P, 2, D], F16)
        wf_l = sb(step3, "wf_l", [P, 2, D], F16)
        fmx = sb(step3, "fmx", [P, OT + 1], F32)
        s_pk = [sem(f"packed_loaded{k}") for k in range(2)]
        s_zs = sem("zero_scale_loaded")
        s_nib = sem("nibbles_ready")
        s_g = sem("unpacked_ready")
        s_fc = sem("ffn_small_done")
        s_fm = sem("ffn_max_ready")
        s_fa = sem("ffn_max_all_ready")
        s_fu = sem("ffn_scale_ready")
        s_fh = sem("ffn_high_ready")
        s_fl = sem("ffn_low_ready")
        s_ft = sem("ffn_transposed")
        s_fth = sem("ffn_high_stored")
        s_ftl = sem("ffn_low_stored")
        with nc.Block("unpack") as block:
            @block.sync
            def _(sp):
                sp.dma_start(zs[:, 0], w_zero.rearrange("(t p g) -> p t g", p=P, g=NG)).then_inc(s_zs, 16)
                sp.dma_start(zs[:, 1], w_scale.rearrange("(t p g) -> p t g", p=P, g=NG)).then_inc(s_zs, 16)
                view = w_packed.rearrange("(t p n) -> t p n", p=P, n=D // 2)
                for t in range(OT):
                    wait(sp, s_nib, t - 1)
                    sp.dma_start(packed[:, t % 2], view[t]).then_inc(s_pk[t % 2], 16)

            @block.gpsimd
            def _(pool):
                pool.wait_ge(s_fm, 1)
                pool.partition_all_reduce(w_absmax[:, 4:5], fmx[:, OT:OT + 1], P, RMAX).then_inc(s_fa, 1)

            @block.scalar
            def _(act):
                act.wait_ge(s_fu, 1)
                for t in range(OT):
                    wait(act, s_ft, 2 * (t - 1))
                    act.activation(wf_h[:, t % 2], wf[:, t], ACT.Copy, scale=w_up[:, 4:5]).then_inc(s_fh, 1)
                    act.wait_ge(s_ft, 2 * t + 1)
                    act.activation(wfT_h[:, :, t * P:(t + 1) * P],
                                   banks[2 * (t % 2)][:].bitcast(F16).rearrange("p (c s) -> p c s", s=P),
                                   ACT.Copy).then_inc(s_fth, 1)

            @block.vector
            def _(dve):
                done = [0]

                def chain(ins):
                    done[0] += 1
                    ins.then_inc(s_fc, 1)
                    dve.wait_ge(s_fc, done[0])

                dve.wait_ge(s_zs, 32)
                for t in range(OT):
                    k = t % 2
                    dve.wait_ge(s_pk[k], 16 * (t // 2 + 1))
                    nc.vector.tensor_scalar(nib[:, k, 0], packed[:, k], 15, None, ALU.bitwise_and)
                    nc.vector.tensor_scalar(nib[:, k, 1], packed[:, k], 4, None, ALU.arith_shift_right).then_inc(s_nib, 1)
                    dve.wait_ge(s_nib, t + 1)
                    zero = zs[:, 0, t, :].unsqueeze(2).to_broadcast([P, NG, GROUP // 2])
                    scale = zs[:, 1, t, :].unsqueeze(2).to_broadcast([P, NG, GROUP])
                    pairs = wf[:, t].rearrange("p (g m a) -> p a g m", g=NG, a=2)
                    for a in range(2):
                        ins = nc.vector.tensor_tensor(pairs[:, a], nib[:, k, a].rearrange("p (g m) -> p g m", g=NG), zero,
                                                      ALU.subtract)
                    chain(ins)
                    grouped = wf[:, t].rearrange("p (g m) -> p g m", g=NG)
                    chain(nc.vector.tensor_tensor(grouped, grouped, scale, ALU.mult))
                    chain(nc.vector.tensor_reduce(fmx[:, t:t + 1], wf[:, t], AX.X, ALU.max, apply_absolute_value=True))
                nc.vector.tensor_reduce(fmx[:, OT:OT + 1], fmx[:, 0:OT], AX.X, ALU.max).then_inc(s_fm, 1)
                dve.wait_ge(s_fa, 1)
                pow2_scales(dve, chain, 4, 5)
                nc.vector.tensor_scalar(ffn_scale[:], w_down[:, 4:5], 1.0 / XN_SCALE, None, ALU.mult).then_inc(s_fu, 1)
                for t in range(OT):
                    dve.wait_ge(s_fh, t + 1)
                    wait(dve, s_ft, 2 * (t - 1))
                    nc.vector.scalar_tensor_tensor(wf_l[:, t % 2], wf[:, t], w_up[:, 4:5], wf_h[:, t % 2],
                                                   ALU.mult, ALU.subtract).then_inc(s_fl, 1)
                    dve.wait_ge(s_ft, 2 * t + 2)
                    nc.vector.tensor_copy(wfT_l[:, :, t * P:(t + 1) * P],
                                          banks[1 + 2 * (t % 2)][:].bitcast(F16).rearrange("p (c s) -> p c s", s=P)
                                          ).then_inc(s_ftl, 1)

            @block.tensor
            def _(pe):
                for t in range(OT):
                    for part, ready, read, bank in ((wf_h, s_fh, s_fth, 0), (wf_l, s_fl, s_ftl, 1)):
                        pe.wait_ge(ready, t + 1)
                        wait(pe, read, t - 1)
                        dst = banks[bank + 2 * (t % 2)][:].bitcast(F16)
                        for c in range(IC):
                            ins = pe.transpose(dst[:, c * P:(c + 1) * P], part[:, t % 2, c * P:(c + 1) * P], ident[:])
                        ins.then_inc(s_ft, 1)

    step4 = ExitStack()
    with step4:
        KR = 3 * HD
        q_st = sb(step4, "q_st", [P, 4, S], F16)
        k_st = sb(step4, "k_st", [P, 4, S], F16)
        v_st = sb(step4, "v_in", [P, 4, 2, 4 * VW], F16)
        p32 = sb(step4, "p32", [P, UNITS * 512], F32)
        p_h = sb(step4, "p_h", [P, 2, UNITS * 512], F16)
        p_l = sb(step4, "p_l", [P, 2, UNITS * 512], F16)
        neg_id = sb(step4, "neg_id", [P, P], mybir.dt.bfloat16)
        past = sb(step4, "past", [P, 2, P], mybir.dt.bfloat16)
        mx = sb(step4, "mx", [P, NSEG], F32)
        nm = sb(step4, "nm", [P, 2, QT], F32)
        m_row = sb(step4, "m_row", [P, 2 * QT], F16)
        mT = sb(step4, "mT", [2 * QT, 2, P], F16)
        c32 = sb(step4, "c32", [P, QT, VW], F32)
        rsum = sb(step4, "rsum", [P, QT], F32)
        osum = sb(step4, "osum", [P, QT, HD], F32)
        o32 = sb(step4, "o32", [P, QT, 4, HD], F32)
        o_h = sb(step4, "o_h", [P, QT * P], F16)
        o_l = sb(step4, "o_l", [P, QT * P], F16)
        oT_s = sb(step4, "oT_s", [P, 2, QT * P], F16)
        xf = sb(step4, "xf", [P, D], F32)
        y_st = sb(step4, "y_st", [P, D], F32)
        POOL_W = 5 * P

        s_ld = [sem(f"qkv_loaded{k}") for k in range(4)]
        s_const = sem("constants_ready")
        s_mrow = [sem(f"max_rows_loaded{k}") for k in range(4)]
        s_a = sem("score_segment_ready")
        s_max = sem("segment_max_ready")
        s_mc = sem("max_small_done")
        s_mr = sem("max_columns_ready")
        s_mt = sem("max_transposed")
        s_mcp = sem("max_rows_ready")
        s_b = sem("scoresT_unit_ready")
        s_exp = sem("probs_unit_ready")
        s_hi = sem("probs_high_ready")
        s_lo = sem("probs_low_dve_ready")
        s_lop = sem("probs_low_pool_ready")
        s_pv = sem("pv_tile_ready")
        s_c = sem("pv_half_copied")
        s_nc = sem("norm_small_done")
        s_norm = sem("head_normalised")
        s_oh = sem("o_high_ready")
        s_ol = sem("o_low_ready")
        s_ot = sem("o_transposed")
        s_oth = sem("oT_high_stored")
        s_otl = sem("oT_low_stored")
        s_ow = sem("oT_written")
        s_f = sem("ffn_half_ready")
        s_fe = sem("ffn_half_added")
        s_xf = [sem(f"x_half_loaded{k}") for k in range(2)]
        s_yw = [sem(f"y_half_written{k}") for k in range(2)]
        GROUPS = PAIRS // 4

        def rounds(eng, body):
            body(0, True, False)
            with eng.Fori(1, GROUPS - 1) as i:
                body(i, False, False)
            body(GROUPS - 1, False, True)

        with nc.Block("attention") as block:
            @block.sync
            def _(sp):
                def load_pair(i, j):
                    g, k = i + j // 4, j % 4
                    n = held(sp, 4 * i + j)
                    if not (isinstance(i, int) and n < 4):
                        wait(sp, s_pv, QT * (n - 3))
                    q_all = q_scr.rearrange("b h r d s -> (b h) (r d) s")[bass.ds(n, 1)].rearrange("a r s -> (a r) s")
                    k_all = k_scr.rearrange("b h r d s -> (b h) (r d) s")[bass.ds(n, 1)].rearrange("a r s -> (a r) s")
                    sp.dma_start(q_st[0:2 * HD, k], q_all).then_inc(s_ld[k], 16)
                    sp.dma_start(q_st[2 * HD:KR, k], q_all[0:HD]).then_inc(s_ld[k], 16)
                    sp.dma_start(k_st[0:HD, k], k_all[0:HD]).then_inc(s_ld[k], 16)
                    sp.dma_start(k_st[HD:KR, k], k_all).then_inc(s_ld[k], 16)
                    v_all = v_scr.rearrange("b h t p c -> (b h) t p c")[bass.ds(n, 1)].rearrange("a t p c -> p (a t) c")
                    sp.dma_start(v_st[:, k], v_all).then_inc(s_ld[k], 16)

                def max_rows(i, j):
                    n = 4 * i + j
                    wait(sp, s_mcp, n + 1)
                    for r in range(2):
                        sp.dma_start(q_st[KR + r:KR + r + 1, j % 4, :].rearrange("a (t s) -> a t s", s=P),
                                     mT[r * QT:(r + 1) * QT, j % 2, :]).then_inc(s_mrow[j % 4], 16)

                def ffn_half(i, hf):
                    cs = slice(512 * hf, 512 * hf + 512)
                    last = i if hf == 0 else held(sp, i - 1)
                    nxt = held(sp, last + 1)
                    store = not (isinstance(last, int) and last < 0)
                    load = not (isinstance(nxt, int) and nxt >= GROUPS)
                    if store:
                        wait(sp, s_fe, 2 * last + hf + 1)
                    for what in (("load", "store") if hf == 0 else ("store", "load")):
                        if what == "store" and store:
                            sp.dma_start(y_scr[bass.ds(last, 1), :, cs].rearrange("a p c -> (a p) c"),
                                         y_st[:, cs]).then_inc(s_yw[hf], 16)
                        if what == "load" and load:
                            sp.dma_start(xf[:, cs], x_tiles[bass.ds(nxt, 1), :, cs].rearrange("a p c -> (a p) c")
                                         ).then_inc(s_xf[hf], 16)

                load_pair(0, 0)
                load_pair(0, 1)
                sp.dma_start(xf[:, 0:512], x_tiles[0, :, 0:512]).then_inc(s_xf[0], 16)
                max_rows(0, 0)

                def body(i, first, last):
                    for j in range(4):
                        if not (last and j >= 2):
                            load_pair(i, j + 2)
                        if j == 0:
                            ffn_half(i, 1)
                        if j == 2:
                            ffn_half(i, 0)
                        if j == 2:
                            if not first:
                                store_group(i - 1)
                        if not (last and j == 3):
                            max_rows(i, j + 1)

                def store_group(g):
                    g = held(sp, g)
                    count = held(sp, g + 1)
                    wait(sp, s_oth, count)
                    wait(sp, s_otl, count)
                    sp.dma_start(o_scr[bass.ds(g, 1)].rearrange("a p r s -> (a p) r s"), oT_s[:]).then_inc(s_ow, 16)

                rounds(sp, body)
                ffn_half(GROUPS, 1)
                store_group(GROUPS - 1)
                sp.wait_ge(s_ow, 16 * GROUPS)
                for hf in range(2):
                    sp.wait_ge(s_yw[hf], 16 * GROUPS)

            @block.gpsimd
            def _(pool):
                pool.memset(neg_id[:], 0.0).then_inc(s_const, 1)
                pool.memset(past[:], MASKED).then_inc(s_const, 1)
                pool.wait_ge(s_const, 2)
                pool.affine_select(out=neg_id[:], in_=neg_id[:], compare_op=ALU.not_equal, fill=-MASKED,
                                   base=0, pattern=[[-1, P]], channel_multiplier=1).then_inc(s_const, 1)
                for side in range(2):
                    sign = 1 - 2 * side
                    pool.affine_select(out=past[:, side], in_=past[:, side], compare_op=ALU.is_gt, fill=0.0, base=0,
                                       pattern=[[sign, P]], channel_multiplier=-sign).then_inc(s_const, 1)
                pool.wait_ge(s_const, 5)
                pool.memset(k_st[KR:KR + 2, :, :], 1.0 / MAX_SCALE).then_inc(s_const, 1)

                def body(i, first, last):
                    for j in range(4):
                        n = 4 * i + j
                        for c in range(CHUNKS):
                            cs = slice((c + 1) * CW - POOL_W, (c + 1) * CW)
                            wait(pool, s_hi, CHUNKS * n + c + 1)
                            nc.gpsimd.tensor_tensor(p_l[:, j % 2, cs], p32[:, cs], p_h[:, j % 2, cs],
                                                    ALU.subtract).then_inc(s_lop, 1)
                rounds(pool, body)

            @block.scalar
            def _(act):
                def copy_rows(i, j):
                    n = 4 * i + j
                    wait(act, s_mt, n + 1)
                    if not (isinstance(i, int) and n < 2):
                        wait(act, s_mrow[(j - 2) % 4], 32 * (i + (j - 2) // 4 + 1))
                    act.activation(mT[:, j % 2, :], banks[7][0:2 * QT].bitcast(F16)[:, 0:P], ACT.Copy).then_inc(s_mcp, 1)

                def copy_pv(i, j, half):
                    n = 4 * i + j
                    wait(act, s_pv, QT * n + 4 * (half + 1))
                    if half == 0:
                        wait(act, s_norm, n)
                    act.activation(c32[:, 4 * half:4 * half + 4, :].rearrange("p t c -> p (t c)"),
                                   banks[4 + half][:, 0:4 * VW], ACT.Copy).then_inc(s_c, 1)

                def group_high(i, j):
                    g = i - 1
                    wait(act, s_norm, 4 * i)
                    wait(act, s_ot, 2 * g)
                    act.activation(o_h[:], o32[:].rearrange("p t h d -> p (t h d)"), ACT.Copy).then_inc(s_oh, 1)

                def group_high_out(i):
                    g = i - 1
                    wait(act, s_ot, 2 * g + 1)
                    wait(act, s_ow, 16 * g)
                    act.activation(oT_s[:, 0], banks[7][:].bitcast(F16), ACT.Copy).then_inc(s_oth, 1)

                copy_rows(0, 0)

                def body(i, first, last):
                    for j in range(4):
                        n = 4 * i + j
                        if j == 1 and not first:
                            group_high(i, j)

                        def exps(u):
                            c = u // CHUNK
                            wait(act, s_b, UNITS * n + u + 1)
                            if u % CHUNK == 0:
                                wait(act, s_hi, CHUNKS * (n - 1) + c + 1)
                                wait(act, s_lo, CHUNKS * (n - 1) + c + 1)
                                wait(act, s_lop, CHUNKS * (n - 1) + c + 1)
                            act.activation(p32[:, 512 * u:512 * u + 512], banks[2 + (u + j) % 2][:], ACT.Exp,
                                           scale=exp_scale[:]).then_inc(s_exp, 1)

                        def high(c):
                            wait(act, s_exp, UNITS * n + CHUNK * (c + 1))
                            if c == 0:
                                wait(act, s_pv, QT * (n - 1))
                            act.activation(p_h[:, j % 2, c * CW:(c + 1) * CW], p32[:, c * CW:(c + 1) * CW],
                                           ACT.Copy).then_inc(s_hi, 1)

                        for u in range(3):
                            exps(u)
                        high(0)
                        if j == 1 and not first:
                            group_high_out(i)
                        if not (first and j == 0):
                            copy_pv(i, j - 1, 0)
                        for u in range(3, 6):
                            exps(u)
                        high(1)
                        if not (first and j == 0):
                            copy_pv(i, j - 1, 1)
                        for u in range(6, 9):
                            exps(u)
                        high(2)
                        if not (last and j == 3):
                            copy_rows(i, j + 1)
                rounds(act, body)
                copy_pv(GROUPS - 1, 3, 0)
                copy_pv(GROUPS - 1, 3, 1)
                group_high(GROUPS, 1)
                group_high_out(GROUPS)

            @block.vector
            def _(dve):

                def seg_max(i, j, s):
                    n = 4 * i + j
                    t, k0, w, diagonal = SEGMENTS[s]
                    wait(dve, s_a, NSEG * n + s + 1)
                    src = banks[s % 2][:, 0:w]
                    nc.vector.tensor_reduce(mx[:, s:s + 1], src, AX.X, ALU.max).then_inc(s_max, 1)

                def max_columns(i, j):
                    n = 4 * i + j
                    wait(dve, s_max, NSEG * (n + 1))
                    nc.vector.tensor_copy(nm[:, 0, 0:4], mx[:, 4:8])
                    nc.vector.tensor_tensor(nm[:, 0, 4:8], mx[:, 0:4], mx[:, 8:12], ALU.max).then_inc(s_mc, 1)
                    wait(dve, s_mc, 3 * n + 1)
                    nc.vector.tensor_scalar(nm[:, 1], nm[:, 0], -MAX_SCALE, None, ALU.mult).then_inc(s_mc, 1)
                    wait(dve, s_mc, 3 * n + 2)
                    wait(dve, s_mt, n)
                    nc.vector.tensor_copy(m_row[:, 0:QT], nm[:, 1]).then_inc(s_mc, 1)
                    wait(dve, s_mc, 3 * n + 3)
                    nc.vector.tensor_tensor(m_row[:, QT:2 * QT], nm[:, 1], m_row[:, 0:QT], ALU.subtract).then_inc(s_mr, 1)

                def low(i, j, c):
                    n = 4 * i + j
                    cs = slice(c * CW, (c + 1) * CW - POOL_W)
                    wait(dve, s_hi, CHUNKS * n + c + 1)
                    nc.vector.tensor_tensor(p_l[:, j % 2, cs], p32[:, cs], p_h[:, j % 2, cs], ALU.subtract).then_inc(s_lo, 1)

                def normalise(i, j):
                    n = 4 * i + j
                    wait(dve, s_c, 2 * n + 2)
                    nc.vector.reciprocal(rsum[:], c32[:, :, 2 * HD])
                    nc.vector.tensor_tensor(osum[:], c32[:, :, 0:HD], c32[:, :, HD:2 * HD], ALU.add).then_inc(s_nc, 1)
                    wait(dve, s_nc, n + 1)
                    nc.vector.tensor_tensor(o32[:, :, j % 4, :], osum[:], rsum[:].unsqueeze(2).to_broadcast([P, QT, HD]),
                                            ALU.mult).then_inc(s_norm, 1)

                def group_low(i):
                    wait(dve, s_oh, i)
                    nc.vector.tensor_tensor(o_l[:], o32[:].rearrange("p t h d -> p (t h d)"), o_h[:],
                                            ALU.subtract).then_inc(s_ol, 1)

                def group_low_out(i):
                    g = i - 1
                    wait(dve, s_ot, 2 * i)
                    wait(dve, s_ow, 16 * g)
                    nc.vector.tensor_copy(oT_s[:, 1], banks[7][:].bitcast(F16)).then_inc(s_otl, 1)

                def ffn_add(i, hf):
                    cs = slice(512 * hf, 512 * hf + 512)
                    wait(dve, s_f, 2 * i + hf + 1)
                    wait(dve, s_xf[hf], 16 * (i + 1))
                    wait(dve, s_yw[hf], 16 * i)
                    nc.vector.scalar_tensor_tensor(y_st[:, cs], banks[6][:], ffn_scale[:], xf[:, cs],
                                                   ALU.mult, ALU.add).then_inc(s_fe, 1)

                for s in range(NSEG):
                    seg_max(0, 0, s)
                max_columns(0, 0)

                def body(i, first, last):
                    for j in range(4):
                        ahead = not (last and j == 3)
                        if j == 1 and not first:
                            group_low(i)
                        if j in (0, 2) and not (first and j == 0):
                            ffn_add(i - 1 if j == 0 else i, 1 if j == 0 else 0)
                        for s in range(0, 4):
                            if ahead:
                                seg_max(i, j + 1, s)
                        low(i, j, 0)
                        if j == 1 and not first:
                            group_low_out(i)
                        for s in range(4, 8):
                            if ahead:
                                seg_max(i, j + 1, s)
                        low(i, j, 1)
                        for s in range(8, NSEG):
                            if ahead:
                                seg_max(i, j + 1, s)
                        if ahead:
                            max_columns(i, j + 1)
                        if not (first and j == 0):
                            normalise(i, j - 1)
                        low(i, j, 2)
                rounds(dve, body)
                ffn_add(GROUPS - 1, 1)
                normalise(GROUPS - 1, 3)
                group_low(GROUPS)
                group_low_out(GROUPS)

            @block.tensor
            def _(pe):
                pe.wait_ge(s_const, 6)

                def segment(i, j, s):
                    n, k = 4 * i + j, j % 4
                    t, k0, w, diagonal = SEGMENTS[s]
                    if s == 0:
                        wait(pe, s_ld[k], 80 * (i + j // 4 + 1))
                    wait(pe, s_max, NSEG * n + s - 1)
                    ins = pe.matmul(banks[s % 2][:, 0:w], q_st[0:KR, k, t * P:(t + 1) * P], k_st[0:KR, k, k0:k0 + w],
                                    start=True, stop=not diagonal)
                    if diagonal:
                        ins = pe.matmul(banks[s % 2][:, w - P:w], neg_id[:], past[:, 0], start=False, stop=True)
                    ins.then_inc(s_a, 1)

                def unit(i, j, u):
                    n, k = 4 * i + j, j % 4
                    if u == 0:
                        wait(pe, s_mrow[k], 32 * (i + 1))
                    wait(pe, s_exp, UNITS * n + u - 1)
                    acc = banks[2 + (u + j) % 2]
                    for col, kt, t, tiles in unit_runs(u):
                        diagonal = t == kt
                        ins = pe.matmul(acc[:, col:col + tiles * P], k_st[0:KR + 2, k, kt * P:(kt + 1) * P],
                                        q_st[0:KR + 2, k, t * P:(t + tiles) * P], start=True, stop=not diagonal)
                        if diagonal:
                            ins = pe.matmul(acc[:, col:col + P], neg_id[:], past[:, 1], start=False, stop=True)
                    ins.then_inc(s_b, 1)

                def pv(i, j, t):
                    n, k = 4 * i + j, j % 4
                    if t == 0:
                        wait(pe, s_hi, CHUNKS * (n + 1))
                        wait(pe, s_lo, CHUNKS * (n + 1))
                        wait(pe, s_lop, CHUNKS * (n + 1))
                    if t % 4 == 0:
                        wait(pe, s_c, 2 * (n - 1) + t // 4 + 1)
                    acc = banks[4 + t // 4][:, (t % 4) * VW:(t % 4 + 1) * VW]
                    for kt in range(t + 1):
                        at = SLOT[(kt, t)] * P
                        v = v_st[:, k, kt // 4, (kt % 4) * VW:(kt % 4 + 1) * VW]
                        pe.matmul(acc, p_h[:, j % 2, at:at + P], v, start=(kt == 0), stop=False)
                        ins = pe.matmul(acc, p_l[:, j % 2, at:at + P], v, start=False, stop=(kt == t))
                    ins.then_inc(s_pv, 1)

                def transpose_max(i, j, after_group):
                    n = 4 * i + j
                    wait(pe, s_mr, n + 1)
                    wait(pe, s_mcp, n)
                    if after_group:
                        wait(pe, s_otl, i)
                    pe.transpose(banks[7][0:2 * QT].bitcast(F16)[:, 0:P], m_row[:], ident[:]).then_inc(s_mt, 1)

                def transpose_group(i, part):
                    src = (o_h, o_l)[part]
                    wait(pe, (s_oh, s_ol)[part], i)
                    if part == 0:
                        wait(pe, s_mcp, 4 * i + 2 if not (isinstance(i, int) and i == GROUPS) else PAIRS)
                    else:
                        wait(pe, s_oth, i)
                    for t in range(QT):
                        ins = pe.transpose(banks[7][:].bitcast(F16)[:, t * P:(t + 1) * P], src[:, t * P:(t + 1) * P], ident[:])
                    ins.then_inc(s_ot, 1)

                def ffn(i, j):
                    hf = j // 2
                    if j % 2 == 0:
                        wait(pe, s_fe, 2 * i + hf)
                    for c in range(4 * (j % 2), 4 * (j % 2) + 4):
                        at = bass.ds(i * P, P)
                        cs = slice(512 * hf, 512 * hf + 512)
                        pe.matmul(banks[6][:], xnT_h[:, c, at], wfT_h[:, c, cs], start=(c == 0), stop=False)
                        pe.matmul(banks[6][:], xnT_h[:, c, at], wfT_l[:, c, cs], start=False, stop=False)
                        ins = pe.matmul(banks[6][:], xnT_l[:, c, at], wfT_h[:, c, cs], start=False, stop=(c == IC - 1))
                        yield
                    if j % 2 == 1:
                        ins.then_inc(s_f, 1)
                    yield

                for s in range(NSEG):
                    segment(0, 0, s)
                transpose_max(0, 0, False)

                def body(i, first, last):
                    for j in range(4):
                        ahead = not (last and j == 3)
                        behind = not (first and j == 0)
                        filler = ffn(i, j)
                        if j == 1 and not first:
                            transpose_group(i, 0)
                        for u in range(UNITS):
                            unit(i, j, u)
                            if ahead:
                                segment(i, j + 1, u)
                            if behind and u < QT:
                                pv(i, j - 1, u)
                            if u in (1, 3, 5, 7):
                                next(filler)
                            if u == 4 and j == 1 and not first:
                                transpose_group(i, 1)
                        if ahead:
                            for s in range(UNITS, NSEG):
                                segment(i, j + 1, s)
                        next(filler)
                        if ahead:
                            transpose_max(i, j + 1, j == 1 and not first)
                rounds(pe, body)
                for t in range(QT):
                    pv(GROUPS - 1, 3, t)
                transpose_group(GROUPS, 0)
                transpose_group(GROUPS, 1)

    step5 = ExitStack()
    with step5:
        wo_raw = sb(step5, "wo_raw", [P, IC, D], F32)
        wo_h = sb(step5, "wo_h", [P, IC, D], F16)
        wo_l = sb(step5, "wo_l", [P, IC, D], F16)
        y_in = sb(step5, "y_in", [P, 2, D], F32)
        y_out = sb(step5, "y_out", [P, 2, D], F32)
        oT = (xnT_h, xnT_l)
        s_wo = [sem(f"wo_loaded{c}") for c in range(4)]
        s_oT = [sem(f"oT_loaded{c}") for c in range(4)]
        s_woh = sem("wo_high_ready")
        s_wol = sem("wo_low_ready")
        s_y = [sem(f"y_loaded{k}") for k in range(2)]
        s_op = sem("out_product_ready")
        s_add = sem("out_added")
        s_out = [sem(f"out_written{k}") for k in range(2)]
        with nc.Block("project") as block:
            @block.sync
            def _(sp):
                view = wo.rearrange("(c p) n -> p c n", p=P)
                for c in range(4):
                    sp.dma_start(wo_raw[:, 2 * c:2 * c + 2, :], view[:, 2 * c:2 * c + 2, :]).then_inc(s_wo[c], 16)
                for c in range(4):
                    for r in range(2):
                        src = o_scr[IC * (c // 2):IC * (c // 2 + 1), :, r, 512 * (c % 2):512 * (c % 2) + 512]
                        sp.dma_start(oT[r][:, :, 512 * c:512 * c + 512], src.rearrange("c p s -> p c s")).then_inc(s_oT[c], 16)
                for k in range(2):
                    sp.dma_start(y_in[:, k], y_scr[k]).then_inc(s_y[k], 16)

                def body(i, last):
                    for k in range(2):
                        t = held(sp, 2 * i + k)
                        ahead = held(sp, t + 2)
                        wait(sp, s_add, 2 * t + 2)
                        sp.dma_start(out_tiles[bass.ds(t, 1)].rearrange("a p d -> (a p) d"), y_out[:, k]).then_inc(s_out[k], 16)
                        if not last:
                            sp.dma_start(y_in[:, k], y_scr[bass.ds(ahead, 1)].rearrange("a p d -> (a p) d")).then_inc(s_y[k], 16)
                with sp.Fori(0, TT // 2 - 1) as i:
                    body(i, False)
                body(TT // 2 - 1, True)
                for k in range(2):
                    sp.wait_ge(s_out[k], 16 * TT // 2)

            @block.scalar
            def _(act):
                for c in range(IC):
                    act.wait_ge(s_wo[c // 2], 16)
                    act.activation(wo_h[:, c, :], wo_raw[:, c, :], ACT.Copy, scale=w_up[:, 3:4]).then_inc(s_woh, 1)

            @block.vector
            def _(dve):
                for c in range(IC):
                    dve.wait_ge(s_woh, c + 1)
                    nc.vector.scalar_tensor_tensor(wo_l[:, c, :], wo_raw[:, c, :], w_up[:, 3:4], wo_h[:, c, :],
                                                   ALU.mult, ALU.subtract).then_inc(s_wol, 1)

                def body(i, first):
                    for k in range(2):
                        t = 2 * i + k
                        for n in range(2):
                            cs = slice(512 * n, 512 * n + 512)
                            wait(dve, s_op, 2 * t + n + 1)
                            if n == 0:
                                wait(dve, s_y[k], 16 * (i + 1))
                                if not first:
                                    wait(dve, s_out[k], 16 * i)
                            nc.vector.scalar_tensor_tensor(y_out[:, k, cs], banks[2 * k + n][:], attn_scale[:],
                                                           y_in[:, k, cs], ALU.mult, ALU.add).then_inc(s_add, 1)
                body(0, True)
                with dve.Fori(1, TT // 2) as i:
                    body(i, False)

            @block.tensor
            def _(pe):
                pe.wait_ge(s_woh, IC)
                pe.wait_ge(s_wol, IC)
                for c in range(4):
                    pe.wait_ge(s_oT[c], 32)

                def body(i, first):
                    for k in range(2):
                        t = 2 * i + k
                        for n in range(2):
                            if not first:
                                wait(pe, s_add, 2 * (t - 2) + n + 1)
                            acc = banks[2 * k + n]
                            cs = slice(512 * n, 512 * n + 512)
                            at = bass.ds(t * P, P)
                            for c in range(IC):
                                pe.matmul(acc[:], oT[0][:, c, at], wo_h[:, c, cs], start=(c == 0), stop=False)
                                pe.matmul(acc[:], oT[0][:, c, at], wo_l[:, c, cs], start=False, stop=False)
                                ins = pe.matmul(acc[:], oT[1][:, c, at], wo_h[:, c, cs], start=False, stop=(c == IC - 1))
                            ins.then_inc(s_op, 1)
                body(0, True)
                with pe.Fori(1, TT // 2) as i:
                    body(i, False)


_INS = ["L0_attn_x", "L0_attn_wq", "L0_attn_wk", "L0_attn_wv", "L0_attn_wo", "L0_ffn_W_q", "L0_ffn_scale", "L0_ffn_zero"]


def kernel(**inputs):
    import numpy as _np
    import concourse.bacc as _bacc
    from concourse import mybir as _mybir
    from concourse.bass_utils import run_bass_kernel_spmd as _run

    nc = _bacc.Bacc("TRN2", target_bir_lowering=False, num_devices=1)
    arrays, args = {}, []

    def give(name, a):
        a = _np.ascontiguousarray(a)
        arrays[name] = a
        args.append(nc.dram_tensor(name, a.shape, _mybir.dt.from_np(a.dtype), kind="ExternalInput").ap())

    for name in _INS:
        give(f"in_{name}", inputs[name])
    inv = 1.0 / 10000.0 ** (_np.arange(0, HD, 2)[:HD // 2].astype(_np.float32) / HD)
    angle = _np.outer(_np.arange(S), inv).astype(_np.float32)
    for name, f in (("cos_table", _np.cos), ("sin_table", _np.sin)):
        give(name, _np.tile(f(angle).T * _np.float32(QK_SCALE), (P // (HD // 2), 1)).astype(_np.float32))
    args.append(nc.dram_tensor("out_0_dram", (B, S, D), F32, kind="ExternalOutput").ap())
    build(nc, *args)
    r = _run(nc, [arrays], core_ids=[0])
    return r.results[0]["out_0_dram"]
```

```python
from contextlib import ExitStack

import concourse.bass as bass
from concourse import mybir

F32 = mybir.dt.float32
F16 = mybir.dt.float16
I32 = mybir.dt.int32
ALU = mybir.AluOpType
ACT = mybir.ActivationFunctionType
AX = mybir.AxisListType
RMAX = bass.bass_isa.ReduceOp.max

P = 128
B, S, D = 2, 1024, 1024
H, HD = 32, 32
TOK = B * S
IC = D // P
TT = TOK // P
QT = S // P
PAIRS = B * H
GROUP = 64
NG = D // GROUP
VW = 2 * HD + 1
EPS = 1e-5

XN_SCALE = 2.0 ** 10
W_TOP = 2.0 ** 14
QK_SCALE = 2.0 ** -23
V_SCALE = 2.0 ** -20
MAX_SCALE = 2.0 ** -15
MASKED = 2.0 ** 60

KEY_ORDER = [0, 1, 7, 2, 6, 3, 5, 4]
BLOCKS = [(j, t) for j in KEY_ORDER for t in range(j, QT)]
SLOT = {jt: n for n, jt in enumerate(BLOCKS)}
UNIT = 4
UNITS = len(BLOCKS) // UNIT
CHUNK = 3
CHUNKS = UNITS // CHUNK
CW = CHUNK * UNIT * P
SEGMENTS = [(t, 0, 512, False) for t in range(4, QT)] + \
           [(t, 0, (t + 1) * P, True) for t in range(4)] + \
           [(t, 512, (t - 3) * P, True) for t in range(4, QT)]
NSEG = len(SEGMENTS)
SEGMENTS_AFTER_UNIT = [(0, 1), (2,), (3,), (4, 5), (6,), (7,), (8, 9), (10,), (11,)]


def unit_runs(u):
    runs = []
    for k in range(UNIT):
        j, t = BLOCKS[u * UNIT + k]
        if runs and runs[-1][1] == j:
            runs[-1][3] += 1
        else:
            runs.append([k * P, j, t, 1])
    return runs


def wait(eng, sem, value):
    if isinstance(value, int) and value <= 0:
        return
    eng.wait_ge(sem, value)


def held(eng, value):
    return value if isinstance(value, int) else eng.snap(value)


def build(nc, x, wq, wk, wv, wo, w_packed, w_scale, w_zero, cos_t, sin_t, out):
    q_scr = nc.dram_tensor("q_scr", (B, H, 2, HD, S), F16, kind="Internal").ap()
    k_scr = nc.dram_tensor("k_scr", (B, H, 2, HD, S), F16, kind="Internal").ap()
    v_scr = nc.dram_tensor("v_scr", (B, H, 2, P, 4 * VW), F16, kind="Internal").ap()
    y_scr = nc.dram_tensor("y_scr", (TT, P, D), F32, kind="Internal").ap()
    o_scr = nc.dram_tensor("o_scr", (B * IC, P, 2, S), F16, kind="Internal").ap()
    x_tiles = x.rearrange("b (t p) d -> (b t) p d", p=P)
    out_tiles = out.rearrange("b (t p) d -> (b t) p d", p=P)

    with ExitStack() as whole:
        def sb(ctx, name, shape, dt):
            return ctx.enter_context(nc.sbuf_tensor(name, shape, dt))

        def sem(name):
            return whole.enter_context(nc.semaphore(name))

        banks = [whole.enter_context(nc.psum_tensor(f"bank{i}", [P, 512], F32)) for i in range(8)]
        ident = sb(whole, "ident", [P, P], F16)
        w_absmax = sb(whole, "w_absmax", [P, 5], F32)
        w_pow2 = sb(whole, "w_pow2", [P, 5], F32)
        w_up = sb(whole, "w_up", [P, 5], F32)
        w_down = sb(whole, "w_down", [P, 5], F32)
        exp_scale = sb(whole, "exp_scale", [P, 1], F32)
        attn_scale = sb(whole, "attn_scale", [P, 1], F32)
        ffn_scale = sb(whole, "ffn_scale", [P, 1], F32)
        xnT_h = sb(whole, "xnT_h", [P, IC, TOK], F16)
        xnT_l = sb(whole, "xnT_l", [P, IC, TOK], F16)

        def pow2_scales(dve, chain, c0, c1):
            cs = slice(c0, c1)
            chain(nc.vector.tensor_scalar(w_pow2[:, cs], w_absmax[:, cs], 1e-30, None, ALU.max))
            chain(nc.vector.tensor_scalar(w_pow2[:, cs].bitcast(I32), w_pow2[:, cs].bitcast(I32),
                                          0x7F800000, None, ALU.bitwise_and))
            chain(nc.vector.reciprocal(w_up[:, cs], w_pow2[:, cs]))
            chain(nc.vector.tensor_scalar(w_up[:, cs], w_up[:, cs], W_TOP, None, ALU.mult))
            chain(nc.vector.tensor_scalar(w_down[:, cs], w_pow2[:, cs], 1.0 / W_TOP, None, ALU.mult))

        step1 = ExitStack()
        with step1:
            GT = 4
            w_raw = sb(step1, "w_raw", [P, IC, D], F32)
            wv_h = sb(step1, "wv_h", [P, IC, D], F16)
            wv_l = sb(step1, "wv_l", [P, IC, D], F16)
            xt = sb(step1, "xt", [P, 2, GT, D], F32)
            xh = sb(step1, "xh", [P, 2, D], F16)
            xl = sb(step1, "xl", [P, 2, D], F16)
            stats = sb(step1, "stats", [P, GT, 2, 6], F32)
            mv = sb(step1, "mv", [P, GT, 2], F32)
            sd = sb(step1, "sd", [P, GT], F32)
            ve = sb(step1, "ve", [P, GT], F32)
            rstd = sb(step1, "rstd", [P, GT], F32)
            tmp = sb(step1, "tmp", [P, GT], F32)
            shift = sb(step1, "shift", [P, GT], F32)
            v_st = sb(step1, "v_st", [P, 2, H, GT * VW], F16)
            wmx = sb(step1, "wmx", [P, 16], F32)

            s_id = sem("ident_ready")
            s_wv = [sem(f"wv_loaded{c}") for c in range(4)]
            s_bg = [sem(f"weight_loaded{c}") for c in range(4)]
            s_x = [sem(f"x_loaded{k}") for k in range(2)]
            s_chain = sem("dve_small_done")
            s_wmax = sem("wv_max_ready")
            s_wall = sem("wv_max_all_ready")
            s_wup = sem("wv_scale_ready")
            s_wh = sem("wv_high_ready")
            s_wl = sem("wv_low_ready")
            s_var = sem("variance_ready")
            s_sd = sem("deviation_ready")
            s_rs = sem("rstd_ready")
            s_xn = sem("xn_ready")
            s_xh = sem("xn_high_ready")
            s_xl = sem("xn_low_ready")
            s_tr = sem("xn_transposed")
            s_th = sem("xnT_high_stored")
            s_tl = sem("xnT_low_stored")
            s_v = sem("v_product_ready")
            s_vh = sem("v_high_ready")
            s_vl = sem("v_low_ready")
            s_vw = [sem(f"v_written{k}") for k in range(2)]
            s_bgm = sem("weight_slab_reduced")
            s_all4 = sem("weight_max_all_ready")
            NT1 = TT // GT
            slabs = [(w, c) for w in (wq, wk, wo) for c in range(4)]
            slab_view = [w.rearrange("(c p) n -> p c n", p=P)[:, 2 * c:2 * c + 2, :] for w, c in slabs]

            with nc.Block("norm_v") as block:
                @block.sync
                def _(sp):
                    wv_view = wv.rearrange("(c p) n -> p c n", p=P)
                    for c in range(4):
                        sp.dma_start(w_raw[:, 2 * c:2 * c + 2, :], wv_view[:, 2 * c:2 * c + 2, :]).then_inc(s_wv[c], 16)
                    for k in range(2):
                        sp.dma_start(xt[:, k], x_tiles[GT * k:GT * k + GT].rearrange("t p d -> p t d")).then_inc(s_x[k], 16)
                    wait(sp, s_wh, IC)
                    wait(sp, s_wl, IC)
                    for n in range(12):
                        if n >= 4:
                            wait(sp, s_bgm, n - 3)
                        sp.dma_start(w_raw[:, 2 * (n % 4):2 * (n % 4) + 2, :], slab_view[n]).then_inc(s_bg[n % 4], 16)
                        if n % 6 == 5:
                            k = n // 6
                            wait(sp, s_xl, GT * (k + 1))
                            sp.dma_start(xt[:, k], x_tiles[GT * (k + 2):GT * (k + 3)].rearrange("t p d -> p t d")).then_inc(s_x[k], 16)

                @block.gpsimd
                def _(pool):
                    pool.memset(ident[:], 0.0).then_inc(s_id, 1)
                    pool.wait_ge(s_id, 1)
                    pool.affine_select(out=ident[:], in_=ident[:], compare_op=ALU.not_equal, fill=1.0, base=0,
                                       pattern=[[-1, P]], channel_multiplier=1).then_inc(s_id, 1)
                    for k in range(2):
                        for h in range(GT):
                            pool.memset(v_st[:, k, :, (h + 1) * VW - 1:(h + 1) * VW], 1.0).then_inc(s_id, 1)
                    pool.wait_ge(s_wmax, 1)
                    pool.partition_all_reduce(w_absmax[:, 2:3], wmx[:, 4:5], P, RMAX).then_inc(s_wall, 1)
                    for it in range(NT1):
                        wait(pool, s_vh, 8 * (it + 1))
                        wait(pool, s_vl, 8 * (it + 1))
                        if it == 0:
                            pool.wait_ge(s_id, 2 + 2 * GT)
                        pool.dma_start(v_scr[it // 2, :, it % 2].rearrange("h p c -> p h c"), v_st[:, it % 2]).then_inc(s_vw[it % 2], 16)
                    pool.wait_ge(s_bgm, 13)
                    pool.partition_all_reduce(wmx[:, 13:16], wmx[:, 13:16], P, RMAX).then_inc(s_all4, 1)
                    for k in range(2):
                        wait(pool, s_vw[k], 32)

                @block.scalar
                def _(act):
                    act.wait_ge(s_wup, 1)
                    for c in range(IC):
                        act.activation(wv_h[:, c, :], w_raw[:, c, :], ACT.Copy, scale=w_up[:, 2:3]).then_inc(s_wh, 1)

                    def v_high(t):
                        for n in range(2):
                            wait(act, s_v, 2 * t + n + 1)
                            k, r = (t // GT) % 2, t % GT
                            if t >= 2 * GT and n == 0 and r == 0:
                                wait(act, s_vw[k], 16)
                            act.activation(v_st[:, k, 16 * n:16 * n + 16, r * VW:r * VW + HD],
                                           banks[4 + 2 * (t % 2) + n][:].rearrange("p (h d) -> p h d", d=HD),
                                           ACT.Copy, scale=V_SCALE).then_inc(s_vh, 1)

                    for it in range(NT1):
                        act.wait_ge(s_var, it + 1)
                        act.activation(sd[:], ve[:], ACT.Sqrt).then_inc(s_sd, 1)
                        act.wait_ge(s_rs, it + 1)
                        for r in range(GT):
                            t = it * GT + r
                            wait(act, s_tr, 2 * (t - 1))
                            act.activation(xh[:, t % 2], xt[:, it % 2, r], ACT.Identity, bias=shift[:, r:r + 1],
                                           scale=rstd[:, r:r + 1]).then_inc(s_xh, 1)
                            act.wait_ge(s_tr, 2 * t + 1)
                            act.activation(xnT_h[:, :, t * P:(t + 1) * P],
                                           banks[0 + 2 * (t % 2)][:].bitcast(F16).rearrange("p (c s) -> p c s", s=P),
                                           ACT.Copy).then_inc(s_th, 1)
                            if t >= 1:
                                v_high(t - 1)
                    v_high(TT - 1)

                @block.vector
                def _(dve):
                    done = [0]

                    def chain(ins):
                        done[0] += 1
                        ins.then_inc(s_chain, 1)
                        dve.wait_ge(s_chain, done[0])

                    for c in range(4):
                        dve.wait_ge(s_wv[c], 16)
                        chain(nc.vector.tensor_reduce(wmx[:, c:c + 1], w_raw[:, 2 * c:2 * c + 2, :], AX.XY, ALU.max,
                                                      apply_absolute_value=True))
                    nc.vector.tensor_reduce(wmx[:, 4:5], wmx[:, 0:4], AX.X, ALU.max).then_inc(s_wmax, 1)

                    def split_wv():
                        dve.wait_ge(s_wall, 1)
                        pow2_scales(dve, chain, 2, 3)
                        chain(nc.vector.tensor_copy(tmp[:, 0:1], w_up[:, 2:3]))
                        nc.vector.tensor_copy(tmp[:, 1:2], w_up[:, 2:3]).then_inc(s_wup, 1)
                        for c in range(IC):
                            dve.wait_ge(s_wh, c + 1)
                            nc.vector.scalar_tensor_tensor(wv_l[:, c, :], w_raw[:, c, :], w_up[:, 2:3], wv_h[:, c, :],
                                                           ALU.mult, ALU.subtract).then_inc(s_wl, 1)

                    def v_low(t):
                        for n in range(2):
                            dve.wait_ge(s_vh, 2 * t + n + 1)
                            k, r = (t // GT) % 2, t % GT
                            nc.vector.scalar_tensor_tensor(
                                v_st[:, k, 16 * n:16 * n + 16, r * VW + HD:r * VW + 2 * HD],
                                banks[4 + 2 * (t % 2) + n][:].rearrange("p (h d) -> p h d", d=HD), V_SCALE,
                                v_st[:, k, 16 * n:16 * n + 16, r * VW:r * VW + HD],
                                ALU.mult, ALU.subtract).then_inc(s_vl, 1)

                    slab = [0]

                    def slab_max():
                        n = slab[0]
                        if n < 12:
                            slab[0] += 1
                            dve.wait_ge(s_bg[n % 4], 16 * (n // 4 + 1))
                            nc.vector.tensor_reduce(wmx[:, n:n + 1], w_raw[:, 2 * (n % 4):2 * (n % 4) + 2, :], AX.XY,
                                                    ALU.max, apply_absolute_value=True).then_inc(s_bgm, 1)

                    for it in range(NT1):
                        dve.wait_ge(s_x[it % 2], 16 * (it // 2 + 1))
                        for r in range(GT):
                            for k in range(2):
                                ins = nc.vector.bn_stats(stats[:, r, k, :], xt[:, it % 2, r, 512 * k:512 * k + 512])
                        chain(ins)
                        for r in range(GT):
                            ins = nc.vector.bn_aggr(mv[:, r, :], stats[:, r, :, :].rearrange("p a b -> p (a b)"))
                        chain(ins)
                        if it == 0:
                            split_wv()
                        nc.vector.tensor_scalar(ve[:], mv[:, :, 1], EPS, None, ALU.add).then_inc(s_var, 1)
                        dve.wait_ge(s_var, it + 1)
                        dve.wait_ge(s_sd, it + 1)
                        chain(nc.vector.reciprocal(rstd[:], sd[:]))
                        chain(nc.vector.tensor_tensor(tmp[:], ve[:], rstd[:], ALU.mult))
                        chain(nc.vector.tensor_tensor(tmp[:], tmp[:], rstd[:], ALU.mult))
                        chain(nc.vector.tensor_scalar(tmp[:], tmp[:], -0.5, 1.5, ALU.mult, ALU.add))
                        chain(nc.vector.tensor_scalar(tmp[:], tmp[:], XN_SCALE, None, ALU.mult))
                        chain(nc.vector.tensor_tensor(rstd[:], rstd[:], tmp[:], ALU.mult))
                        chain(nc.vector.tensor_tensor(tmp[:], mv[:, :, 0], rstd[:], ALU.mult))
                        nc.vector.tensor_scalar(shift[:], tmp[:], -1.0, None, ALU.mult).then_inc(s_rs, 1)
                        dve.wait_ge(s_rs, it + 1)
                        for r in range(GT):
                            t = it * GT + r
                            dve.wait_ge(s_xh, t + 1)
                            chain(nc.vector.tensor_scalar(xt[:, it % 2, r], xt[:, it % 2, r], rstd[:, r:r + 1],
                                                          shift[:, r:r + 1], ALU.mult, ALU.add))
                            wait(dve, s_tr, 2 * (t - 1))
                            nc.vector.tensor_tensor(xl[:, t % 2], xt[:, it % 2, r], xh[:, t % 2],
                                                    ALU.subtract).then_inc(s_xl, 1)
                            dve.wait_ge(s_tr, 2 * t + 2)
                            nc.vector.tensor_copy(xnT_l[:, :, t * P:(t + 1) * P],
                                                  banks[1 + 2 * (t % 2)][:].bitcast(F16).rearrange("p (c s) -> p c s", s=P)
                                                  ).then_inc(s_tl, 1)
                            if t >= 1:
                                v_low(t - 1)
                            slab_max()
                    v_low(TT - 1)
                    dve.wait_ge(s_bgm, 12)
                    for w in range(3):
                        ins = nc.vector.tensor_reduce(wmx[:, 13 + w:14 + w], wmx[:, 4 * w:4 * w + 4], AX.X, ALU.max)
                    ins.then_inc(s_bgm, 1)
                    dve.wait_ge(s_all4, 1)
                    for src, dst in ((13, 0), (14, 1), (15, 3)):
                        chain(nc.vector.tensor_copy(w_absmax[:, dst:dst + 1], wmx[:, src:src + 1]))
                    pow2_scales(dve, chain, 0, 2)
                    pow2_scales(dve, chain, 3, 4)
                    chain(nc.vector.tensor_tensor(exp_scale[:], w_down[:, 0:1], w_down[:, 1:2], ALU.mult))
                    chain(nc.vector.tensor_scalar(exp_scale[:], exp_scale[:], 1.0 / (QK_SCALE * XN_SCALE) ** 2,
                                                  float(HD) ** -0.5, ALU.mult, ALU.mult))
                    chain(nc.vector.tensor_tensor(attn_scale[:], w_down[:, 2:3], w_down[:, 3:4], ALU.mult))
                    chain(nc.vector.tensor_scalar(attn_scale[:], attn_scale[:], 1.0 / (V_SCALE * XN_SCALE), None, ALU.mult))

                @block.tensor
                def _(pe):
                    pe.wait_ge(s_id, 2)

                    def v_product(t):
                        if t == 0:
                            pe.wait_ge(s_wh, IC)
                            pe.wait_ge(s_wl, IC)
                        pe.wait_ge(s_th, t + 1)
                        pe.wait_ge(s_tl, t + 1)
                        for n in range(2):
                            wait(pe, s_vl, 2 * (t - 2) + n + 1)
                            acc = banks[4 + 2 * (t % 2) + n]
                            cols = slice(512 * n, 512 * n + 512)
                            for c in range(IC):
                                hi, lo = xnT_h[:, c, t * P:(t + 1) * P], xnT_l[:, c, t * P:(t + 1) * P]
                                pe.matmul(acc[:], hi, wv_h[:, c, cols], start=(c == 0), stop=False)
                                pe.matmul(acc[:], hi, wv_l[:, c, cols], start=False, stop=False)
                                ins = pe.matmul(acc[:], lo, wv_h[:, c, cols], start=False, stop=(c == IC - 1))
                            ins.then_inc(s_v, 1)

                    for t in range(TT):
                        for part, ready, read, bank in ((xh, s_xh, s_th, 0), (xl, s_xl, s_tl, 1)):
                            pe.wait_ge(ready, t + 1)
                            wait(pe, read, t - 1)
                            dst = banks[bank + 2 * (t % 2)][:].bitcast(F16)
                            for c in range(IC):
                                ins = pe.transpose(dst[:, c * P:(c + 1) * P], part[:, t % 2, c * P:(c + 1) * P], ident[:])
                            ins.then_inc(s_tr, 1)
                        if t >= 1:
                            v_product(t - 1)
                    v_product(TT - 1)

        step2 = ExitStack()
        with step2:
            HG = 8
            NGRP = H // HG
            raw = sb(step2, "qk_raw", [P, 2, IC, 256], F32)
            wh = sb(step2, "qk_wh", [P, 2, IC, 2, P], F16)
            wl = sb(step2, "qk_wl", [P, 2, IC, 2, P], F16)
            cosb = sb(step2, "cosb", [P, S], F32)
            sinb = sb(step2, "sinb", [P, S], F32)
            prod = sb(step2, "prod", [P, 2, 4, 512], F32)
            rot = sb(step2, "rot", [P, 2, 2, 512], F32)
            rh = sb(step2, "rh", [P, 2, 2, 512], F16)
            rl = sb(step2, "rl", [P, 2, 2, 512], F16)
            s_tab = sem("tables_loaded")
            s_raw = [sem(f"qk_weight_loaded{k}") for k in range(2)]
            s_qwh = sem("qk_weight_high")
            s_qwl = sem("qk_weight_low")
            s_ps = sem("qk_product_ready")
            s_pr = sem("rotation_products_ready")
            s_rot = sem("rotated_ready")
            s_rh = sem("rotated_high_ready")
            s_rl = sem("rotated_low_ready")
            s_st = [sem(f"qk_written{k}") for k in range(2)]
            TC = TOK // 512
            CH = 2 * TC

            with nc.Block("qk") as block:
                @block.sync
                def _(sp):
                    sp.dma_start(cosb[:], cos_t).then_inc(s_tab, 16)
                    sp.dma_start(sinb[:], sin_t).then_inc(s_tab, 16)
                    views = [w.rearrange("(c p) n -> p c n", p=P) for w in (wq, wk)]

                    def load(g):
                        for w in range(2):
                            if not isinstance(g, int) or g > 0:
                                wait(sp, s_qwl, 2 * (g - 1) + w + 1)
                            sp.dma_start(raw[:, w], views[w][:, :, bass.ds(g * 256, 256)]).then_inc(s_raw[w], 16)

                    load(0)
                    with sp.Fori(1, NGRP) as g:
                        load(g)

                def chunk_out(eng, g, w, tc, part, ab, src):
                    scr = q_scr if w == 0 else k_scr
                    dst = scr[tc // 2, :, part, 16 * ab:16 * ab + 16, 512 * (tc % 2):512 * (tc % 2) + 512]
                    return eng.dma_start(dst[bass.ds(g * HG, HG)].rearrange("h i s -> h i s"), src)

                @block.gpsimd
                def _(pool):
                    def group(g):
                        for w in range(2):
                            for tc in range(TC):
                                m = w * TC + tc
                                k = m % 2
                                n = g * CH + m
                                wait(pool, s_pr, n + 1)
                                if m >= 2 or not isinstance(g, int):
                                    wait(pool, s_rl, 2 * (n - 1))
                                nc.gpsimd.tensor_tensor(rot[:, k, 0], prod[:, k, 0], prod[:, k, 1], ALU.subtract).then_inc(s_rot, 1)
                                nc.gpsimd.tensor_tensor(rot[:, k, 1], prod[:, k, 2], prod[:, k, 3], ALU.add).then_inc(s_rot, 1)
                    group(0)
                    with pool.Fori(1, NGRP) as g:
                        group(g)

                @block.scalar
                def _(act):
                    def group(g):
                        first = isinstance(g, int)
                        for w in range(2):
                            wait(act, s_raw[w], 16 * (g + 1))
                            if not first:
                                wait(act, s_ps, (g - 1) * CH + (w + 1) * TC)
                            for ab in range(2):
                                act.activation(wh[:, w, :, ab, :], raw[:, w].rearrange("p c (m a) -> p a c m", a=2)[:, ab],
                                               ACT.Copy, scale=w_up[:, w:w + 1]).then_inc(s_qwh, 1)
                        for w in range(2):
                            for tc in range(TC):
                                m = w * TC + tc
                                k = m % 2
                                n = g * CH + m
                                for ab in range(2):
                                    wait(act, s_rot, 2 * n + ab + 1)
                                    if ab == 0 and (m >= 2 or not first):
                                        wait(act, s_st[k], 64 * (g * (CH // 2) + m // 2))
                                    act.activation(rh[:, k, ab], rot[:, k, ab], ACT.Copy).then_inc(s_rh, 1)
                                wait(act, s_rl, 2 * (n + 1))
                                wait(act, s_rh, 2 * (n + 1))
                                for part, src in ((0, rh), (1, rl)):
                                    for ab in range(2):
                                        chunk_out(act, g, w, tc, part, ab, src[:, k, ab]).then_inc(s_st[k], 16)
                    group(0)
                    with act.Fori(1, NGRP) as g:
                        group(g)
                    for k in range(2):
                        act.wait_ge(s_st[k], 64 * NGRP * CH // 2)

                @block.vector
                def _(dve):
                    def group(g):
                        first = isinstance(g, int)
                        if first:
                            dve.wait_ge(s_tab, 32)
                        for w in range(2):
                            for ab in range(2):
                                wait(dve, s_qwh, 4 * g + 2 * w + ab + 1)
                                for c4 in range(2):
                                    cs = slice(4 * c4, 4 * c4 + 4)
                                    ins = nc.vector.scalar_tensor_tensor(
                                        wl[:, w, cs, ab, :], raw[:, w, cs].rearrange("p c (m a) -> p a c m", a=2)[:, ab],
                                        w_up[:, w:w + 1], wh[:, w, cs, ab, :], ALU.mult, ALU.subtract)
                            ins.then_inc(s_qwl, 1)

                        def rotate(m):
                            k = m % 2
                            n = g * CH + m
                            wait(dve, s_ps, n + 1)
                            if m >= 2 or not first:
                                wait(dve, s_rot, 2 * (n - 1))
                            s0 = 512 * (m % 2)
                            c, s = cosb[:, s0:s0 + 512], sinb[:, s0:s0 + 512]
                            even, odd = banks[2 * k][:], banks[2 * k + 1][:]
                            nc.vector.tensor_tensor(prod[:, k, 0], even, c, ALU.mult)
                            nc.vector.tensor_tensor(prod[:, k, 1], odd, s, ALU.mult)
                            nc.vector.tensor_tensor(prod[:, k, 2], even, s, ALU.mult)
                            nc.vector.tensor_tensor(prod[:, k, 3], odd, c, ALU.mult).then_inc(s_pr, 1)

                        def low(m):
                            k = m % 2
                            n = g * CH + m
                            for ab in range(2):
                                wait(dve, s_rh, 2 * n + ab + 1)
                                nc.vector.tensor_tensor(rl[:, k, ab], rot[:, k, ab], rh[:, k, ab],
                                                        ALU.subtract).then_inc(s_rl, 1)

                        for m in range(CH):
                            rotate(m)
                            if m >= 1:
                                low(m - 1)
                        low(CH - 1)
                    group(0)
                    with dve.Fori(1, NGRP) as g:
                        group(g)

                @block.tensor
                def _(pe):
                    def group(g):
                        first = isinstance(g, int)
                        for w in range(2):
                            wait(pe, s_qwh, 4 * g + 2 * w + 2)
                            wait(pe, s_qwl, 2 * g + w + 1)
                            for tc in range(TC):
                                m = w * TC + tc
                                k = m % 2
                                n = g * CH + m
                                if m >= 2 or not first:
                                    wait(pe, s_pr, n - 1)
                                for ab in range(2):
                                    acc = banks[2 * k + ab]
                                    for c in range(IC):
                                        hi = xnT_h[:, c, 512 * tc:512 * tc + 512]
                                        lo = xnT_l[:, c, 512 * tc:512 * tc + 512]
                                        pe.matmul(acc[:], wh[:, w, c, ab], hi, start=(c == 0), stop=False)
                                        pe.matmul(acc[:], wh[:, w, c, ab], lo, start=False, stop=False)
                                        ins = pe.matmul(acc[:], wl[:, w, c, ab], hi, start=False, stop=(c == IC - 1))
                                ins.then_inc(s_ps, 1)
                    group(0)
                    with pe.Fori(1, NGRP) as g:
                        group(g)

        step3_to_5(nc, whole, sb, sem, banks, ident, xnT_h, xnT_l, w_absmax, w_up, w_down, pow2_scales,
                   exp_scale, attn_scale, ffn_scale, q_scr, k_scr, v_scr, y_scr, o_scr, x_tiles, out_tiles,
                   wo, w_packed, w_scale, w_zero)


def step3_to_5(nc, whole, sb, sem, banks, ident, xnT_h, xnT_l, w_absmax, w_up, w_down, pow2_scales,
               exp_scale, attn_scale, ffn_scale, q_scr, k_scr, v_scr, y_scr, o_scr, x_tiles, out_tiles,
               wo, w_packed, w_scale, w_zero):
    wfT_h = sb(whole, "wfT_h", [P, IC, D], F16)
    wfT_l = sb(whole, "wfT_l", [P, IC, D], F16)

    step3 = ExitStack()
    with step3:
        OT = D // P
        packed = sb(step3, "packed", [P, 2, D // 2], I32)
        nib = sb(step3, "nib", [P, 2, 2, D // 2], I32)
        zs = sb(step3, "zs", [P, 2, OT, NG], F32)
        wf = sb(step3, "wf", [P, OT, D], F32)
        wf_h = sb(step3, "wf_h", [P, 2, D], F16)
        wf_l = sb(step3, "wf_l", [P, 2, D], F16)
        fmx = sb(step3, "fmx", [P, OT + 1], F32)
        s_pk = [sem(f"packed_loaded{k}") for k in range(2)]
        s_zs = sem("zero_scale_loaded")
        s_nib = sem("nibbles_ready")
        s_g = sem("unpacked_ready")
        s_fc = sem("ffn_small_done")
        s_fm = sem("ffn_max_ready")
        s_fa = sem("ffn_max_all_ready")
        s_fu = sem("ffn_scale_ready")
        s_fh = sem("ffn_high_ready")
        s_fl = sem("ffn_low_ready")
        s_ft = sem("ffn_transposed")
        s_fth = sem("ffn_high_stored")
        s_ftl = sem("ffn_low_stored")
        with nc.Block("unpack") as block:
            @block.sync
            def _(sp):
                sp.dma_start(zs[:, 0], w_zero.rearrange("(t p g) -> p t g", p=P, g=NG)).then_inc(s_zs, 16)
                sp.dma_start(zs[:, 1], w_scale.rearrange("(t p g) -> p t g", p=P, g=NG)).then_inc(s_zs, 16)
                view = w_packed.rearrange("(t p n) -> t p n", p=P, n=D // 2)
                for t in range(OT):
                    wait(sp, s_nib, t - 1)
                    sp.dma_start(packed[:, t % 2], view[t]).then_inc(s_pk[t % 2], 16)

            @block.gpsimd
            def _(pool):
                pool.wait_ge(s_fm, 1)
                pool.partition_all_reduce(w_absmax[:, 4:5], fmx[:, OT:OT + 1], P, RMAX).then_inc(s_fa, 1)

            @block.scalar
            def _(act):
                act.wait_ge(s_fu, 1)
                for t in range(OT):
                    wait(act, s_ft, 2 * (t - 1))
                    act.activation(wf_h[:, t % 2], wf[:, t], ACT.Copy, scale=w_up[:, 4:5]).then_inc(s_fh, 1)
                    act.wait_ge(s_ft, 2 * t + 1)
                    act.activation(wfT_h[:, :, t * P:(t + 1) * P],
                                   banks[2 * (t % 2)][:].bitcast(F16).rearrange("p (c s) -> p c s", s=P),
                                   ACT.Copy).then_inc(s_fth, 1)

            @block.vector
            def _(dve):
                done = [0]

                def chain(ins):
                    done[0] += 1
                    ins.then_inc(s_fc, 1)
                    dve.wait_ge(s_fc, done[0])

                dve.wait_ge(s_zs, 32)
                for t in range(OT):
                    k = t % 2
                    dve.wait_ge(s_pk[k], 16 * (t // 2 + 1))
                    nc.vector.tensor_scalar(nib[:, k, 0], packed[:, k], 15, None, ALU.bitwise_and)
                    nc.vector.tensor_scalar(nib[:, k, 1], packed[:, k], 4, None, ALU.arith_shift_right).then_inc(s_nib, 1)
                    dve.wait_ge(s_nib, t + 1)
                    zero = zs[:, 0, t, :].unsqueeze(2).to_broadcast([P, NG, GROUP // 2])
                    scale = zs[:, 1, t, :].unsqueeze(2).to_broadcast([P, NG, GROUP])
                    pairs = wf[:, t].rearrange("p (g m a) -> p a g m", g=NG, a=2)
                    for a in range(2):
                        ins = nc.vector.tensor_tensor(pairs[:, a], nib[:, k, a].rearrange("p (g m) -> p g m", g=NG), zero,
                                                      ALU.subtract)
                    chain(ins)
                    grouped = wf[:, t].rearrange("p (g m) -> p g m", g=NG)
                    chain(nc.vector.tensor_tensor(grouped, grouped, scale, ALU.mult))
                    chain(nc.vector.tensor_reduce(fmx[:, t:t + 1], wf[:, t], AX.X, ALU.max, apply_absolute_value=True))
                nc.vector.tensor_reduce(fmx[:, OT:OT + 1], fmx[:, 0:OT], AX.X, ALU.max).then_inc(s_fm, 1)
                dve.wait_ge(s_fa, 1)
                pow2_scales(dve, chain, 4, 5)
                nc.vector.tensor_scalar(ffn_scale[:], w_down[:, 4:5], 1.0 / XN_SCALE, None, ALU.mult).then_inc(s_fu, 1)
                for t in range(OT):
                    dve.wait_ge(s_fh, t + 1)
                    wait(dve, s_ft, 2 * (t - 1))
                    nc.vector.scalar_tensor_tensor(wf_l[:, t % 2], wf[:, t], w_up[:, 4:5], wf_h[:, t % 2],
                                                   ALU.mult, ALU.subtract).then_inc(s_fl, 1)
                    dve.wait_ge(s_ft, 2 * t + 2)
                    nc.vector.tensor_copy(wfT_l[:, :, t * P:(t + 1) * P],
                                          banks[1 + 2 * (t % 2)][:].bitcast(F16).rearrange("p (c s) -> p c s", s=P)
                                          ).then_inc(s_ftl, 1)

            @block.tensor
            def _(pe):
                for t in range(OT):
                    for part, ready, read, bank in ((wf_h, s_fh, s_fth, 0), (wf_l, s_fl, s_ftl, 1)):
                        pe.wait_ge(ready, t + 1)
                        wait(pe, read, t - 1)
                        dst = banks[bank + 2 * (t % 2)][:].bitcast(F16)
                        for c in range(IC):
                            ins = pe.transpose(dst[:, c * P:(c + 1) * P], part[:, t % 2, c * P:(c + 1) * P], ident[:])
                        ins.then_inc(s_ft, 1)

    step4 = ExitStack()
    with step4:
        KR = 3 * HD
        q_st = sb(step4, "q_st", [P, 4, S], F16)
        k_st = sb(step4, "k_st", [P, 4, S], F16)
        v_st = sb(step4, "v_in", [P, 4, 2, 4 * VW], F16)
        p32 = sb(step4, "p32", [P, UNITS * 512], F32)
        p_h = sb(step4, "p_h", [P, 2, UNITS * 512], F16)
        p_l = sb(step4, "p_l", [P, 2, UNITS * 512], F16)
        neg_id = sb(step4, "neg_id", [P, P], mybir.dt.bfloat16)
        past = sb(step4, "past", [P, 2, P], mybir.dt.bfloat16)
        mx = sb(step4, "mx", [P, 2, QT], F32)
        row_max = sb(step4, "row_max", [P, QT], F32)
        m_row = sb(step4, "m_row", [P, 2 * QT], F16)
        mT = sb(step4, "mT", [2 * QT, 2, P], F16)
        c32 = sb(step4, "c32", [P, QT, VW], F32)
        rsum = sb(step4, "rsum", [P, QT], F32)
        osum = sb(step4, "osum", [P, QT, HD], F32)
        o32 = sb(step4, "o32", [P, QT, 4, HD], F32)
        o_h = sb(step4, "o_h", [P, QT * P], F16)
        o_l = sb(step4, "o_l", [P, QT * P], F16)
        oT_s = sb(step4, "oT_s", [P, 2, QT * P], F16)
        xf = sb(step4, "xf", [P, D], F32)
        y_st = sb(step4, "y_st", [P, D], F32)
        POOL_W = 10 * P
        a_bank = [banks[0], banks[1], banks[5]]
        b_bank = [banks[2], banks[3], banks[7]]
        turn_bank, ffn_bank = banks[4], banks[6]

        s_ld = [sem(f"qk_loaded{k}") for k in range(4)]
        s_ldv = [sem(f"v_loaded{k}") for k in range(4)]
        s_const = sem("constants_ready")
        s_mrow = [sem(f"max_rows_loaded{k}") for k in range(4)]
        s_a = sem("score_segment_ready")
        s_max = sem("segment_max_ready")
        s_mc = sem("max_small_done")
        s_mr = sem("max_columns_ready")
        s_mt = sem("max_transposed")
        s_mcp = sem("max_rows_ready")
        s_b = sem("scoresT_unit_ready")
        s_exp = sem("probs_unit_ready")
        s_hi = sem("probs_high_act_ready")
        s_hid = sem("probs_high_dve_ready")
        s_lo = sem("probs_low_dve_ready")
        s_lop = sem("probs_low_pool_ready")
        s_pv = sem("pv_tile_ready")
        s_c = sem("pv_half_copied")
        s_nc = sem("norm_small_done")
        s_norm = sem("head_normalised")
        s_oh = sem("o_high_ready")
        s_ol = sem("o_low_ready")
        s_ot = sem("o_transposed")
        s_oth = sem("oT_high_stored")
        s_otl = sem("oT_low_stored")
        s_ow = sem("oT_written")
        s_f = sem("ffn_half_ready")
        s_fe = sem("ffn_half_added")
        s_xf = [sem(f"x_half_loaded{k}") for k in range(2)]
        s_yw = [sem(f"y_half_written{k}") for k in range(2)]
        GROUPS = PAIRS // 4

        def rounds(eng, body):
            body(0, True, False)
            with eng.Fori(1, GROUPS - 1) as i:
                body(i, False, False)
            body(GROUPS - 1, False, True)

        with nc.Block("attention") as block:
            @block.sync
            def _(sp):
                def load_qk(i, j):
                    k = j % 4
                    n = held(sp, 4 * i + j)
                    if not (isinstance(i, int) and n < 4):
                        wait(sp, s_b, UNITS * (n - 3))
                    q_all = q_scr.rearrange("b h r d s -> (b h) (r d) s")[bass.ds(n, 1)].rearrange("a r s -> (a r) s")
                    k_all = k_scr.rearrange("b h r d s -> (b h) (r d) s")[bass.ds(n, 1)].rearrange("a r s -> (a r) s")
                    sp.dma_start(q_st[0:2 * HD, k], q_all).then_inc(s_ld[k], 16)
                    sp.dma_start(q_st[2 * HD:KR, k], q_all[0:HD]).then_inc(s_ld[k], 16)
                    sp.dma_start(k_st[0:HD, k], k_all[0:HD]).then_inc(s_ld[k], 16)
                    sp.dma_start(k_st[HD:KR, k], k_all).then_inc(s_ld[k], 16)

                def load_v(i, j):
                    k = j % 4
                    n = held(sp, 4 * i + j)
                    if not (isinstance(i, int) and n < 4):
                        wait(sp, s_pv, QT * (n - 3))
                    v_all = v_scr.rearrange("b h t p c -> (b h) t p c")[bass.ds(n, 1)].rearrange("a t p c -> p (a t) c")
                    sp.dma_start(v_st[:, k], v_all).then_inc(s_ldv[k], 16)

                def max_rows(i, j):
                    n = 4 * i + j
                    wait(sp, s_mcp, n + 1)
                    for r in range(2):
                        sp.dma_start(q_st[KR + r:KR + r + 1, j % 4, :].rearrange("a (t s) -> a t s", s=P),
                                     mT[r * QT:(r + 1) * QT, j % 2, :]).then_inc(s_mrow[j % 4], 16)

                def ffn_half(i, hf):
                    cs = slice(512 * hf, 512 * hf + 512)
                    last = i if hf == 0 else held(sp, i - 1)
                    nxt = held(sp, last + 1)
                    store = not (isinstance(last, int) and last < 0)
                    load = not (isinstance(nxt, int) and nxt >= GROUPS)
                    if store:
                        wait(sp, s_fe, 2 * last + hf + 1)
                    for what in (("load", "store") if hf == 0 else ("store", "load")):
                        if what == "store" and store:
                            sp.dma_start(y_scr[bass.ds(last, 1), :, cs].rearrange("a p c -> (a p) c"),
                                         y_st[:, cs]).then_inc(s_yw[hf], 16)
                        if what == "load" and load:
                            sp.dma_start(xf[:, cs], x_tiles[bass.ds(nxt, 1), :, cs].rearrange("a p c -> (a p) c")
                                         ).then_inc(s_xf[hf], 16)

                for j in range(3):
                    load_qk(0, j)
                for j in range(3):
                    load_v(0, j)
                sp.dma_start(xf[:, 0:512], x_tiles[0, :, 0:512]).then_inc(s_xf[0], 16)
                max_rows(0, 0)

                def body(i, first, last):
                    for j in range(4):
                        if j == 0:
                            ffn_half(i, 1)
                        if j == 2:
                            ffn_half(i, 0)
                        if not (last and j >= 1):
                            load_qk(i, j + 3)
                        if not (last and j == 3):
                            max_rows(i, j + 1)
                        if not (last and j >= 1):
                            load_v(i, j + 3)
                        if j == 3 and not first:
                            store_group(i - 1)

                def store_group(g):
                    g = held(sp, g)
                    count = held(sp, g + 1)
                    wait(sp, s_oth, count)
                    wait(sp, s_otl, count)
                    sp.dma_start(o_scr[bass.ds(g, 1)].rearrange("a p r s -> (a p) r s"), oT_s[:]).then_inc(s_ow, 16)

                rounds(sp, body)
                ffn_half(GROUPS, 1)
                store_group(GROUPS - 1)
                sp.wait_ge(s_ow, 16 * (GROUPS + 1))
                for hf in range(2):
                    sp.wait_ge(s_yw[hf], 16 * GROUPS)

            @block.gpsimd
            def _(pool):
                pool.memset(neg_id[:], 0.0).then_inc(s_const, 1)
                pool.memset(past[:], MASKED).then_inc(s_const, 1)
                pool.memset(mx[:, 1, 0:4], -3.0e38).then_inc(s_const, 1)
                pool.wait_ge(s_const, 3)
                pool.affine_select(out=neg_id[:], in_=neg_id[:], compare_op=ALU.not_equal, fill=-MASKED,
                                   base=0, pattern=[[-1, P]], channel_multiplier=1).then_inc(s_const, 1)
                for side in range(2):
                    sign = 1 - 2 * side
                    pool.affine_select(out=past[:, side], in_=past[:, side], compare_op=ALU.is_gt, fill=0.0, base=0,
                                       pattern=[[sign, P]], channel_multiplier=-sign).then_inc(s_const, 1)
                pool.wait_ge(s_const, 6)
                pool.memset(k_st[KR:KR + 2, :, :], 1.0 / MAX_SCALE).then_inc(s_const, 1)
                pool.memset(oT_s[0:1, 0, 0:1], 0.0).then_inc(s_ow, 16)

                def group_low(i):
                    wait(pool, s_oh, i)
                    nc.gpsimd.tensor_tensor(o_l[:], o32[:].rearrange("p t h d -> p (t h d)"), o_h[:],
                                            ALU.subtract).then_inc(s_ol, 1)

                def body(i, first, last):
                    for j in range(4):
                        n = 4 * i + j
                        for c in range(CHUNKS):
                            if c == 2 and j == 1 and not first:
                                group_low(i)
                            cs = slice((c + 1) * CW - POOL_W, (c + 1) * CW)
                            if c < 2:
                                wait(pool, s_hi, 2 * n + c + 1)
                            else:
                                wait(pool, s_hid, n + 1)
                            nc.gpsimd.tensor_tensor(p_l[:, j % 2, cs], p32[:, cs], p_h[:, j % 2, cs],
                                                    ALU.subtract).then_inc(s_lop, 1)
                rounds(pool, body)
                group_low(GROUPS)

            @block.scalar
            def _(act):
                def copy_rows(i, j):
                    n = 4 * i + j
                    wait(act, s_mt, n + 1)
                    if not (isinstance(i, int) and n < 2):
                        wait(act, s_mrow[(j - 2) % 4], 32 * (i + (j - 2) // 4 + 1))
                    act.activation(mT[:, j % 2, :], turn_bank[0:2 * QT].bitcast(F16)[:, 0:P], ACT.Copy).then_inc(s_mcp, 1)

                def copy_pv(i, j, half):
                    n = 4 * i + j
                    wait(act, s_pv, QT * n + 4 * (half + 1))
                    if half == 0:
                        wait(act, s_norm, n)
                    act.activation(c32[:, 4 * half:4 * half + 4, :].rearrange("p t c -> p (t c)"),
                                   turn_bank[:, 0:4 * VW], ACT.Copy).then_inc(s_c, 1)

                def group_high(i):
                    wait(act, s_norm, 4 * i)
                    act.activation(o_h[:], o32[:].rearrange("p t h d -> p (t h d)"), ACT.Copy).then_inc(s_oh, 1)

                def group_out(i, part):
                    wait(act, s_ot, 2 * (i - 1) + part + 1)
                    if part == 0:
                        wait(act, s_ow, 16 * i)
                    act.activation(oT_s[:, part], turn_bank[:].bitcast(F16), ACT.Copy).then_inc((s_oth, s_otl)[part], 1)

                copy_rows(0, 0)

                def body(i, first, last):
                    for j in range(4):
                        n = 4 * i + j

                        def exps(u):
                            c = u // CHUNK
                            wait(act, s_b, UNITS * n + u + 1)
                            if u % CHUNK == 0:
                                if c < 2:
                                    wait(act, s_hi, 2 * (n - 1) + c + 1)
                                else:
                                    wait(act, s_hid, n)
                                wait(act, s_lo, CHUNKS * (n - 1) + c + 1)
                                wait(act, s_lop, CHUNKS * (n - 1) + c + 1)
                            act.activation(p32[:, 512 * u:512 * u + 512], b_bank[u % 3][:], ACT.Exp,
                                           scale=exp_scale[:]).then_inc(s_exp, 1)

                        def high(c):
                            wait(act, s_exp, UNITS * n + CHUNK * (c + 1))
                            if c == 0:
                                wait(act, s_pv, QT * (n - 1))
                            act.activation(p_h[:, j % 2, c * CW:(c + 1) * CW], p32[:, c * CW:(c + 1) * CW],
                                           ACT.Copy).then_inc(s_hi, 1)

                        exps(0)
                        if not (first and j <= 1):
                            copy_pv(i, j - 2, 1)
                        exps(1)
                        exps(2)
                        if not (last and j == 3):
                            copy_rows(i, j + 1)
                        exps(3)
                        high(0)
                        if j in (2, 3) and not first:
                            group_out(i, j - 2)
                        exps(4)
                        exps(5)
                        if not (first and j == 0):
                            copy_pv(i, j - 1, 0)
                        exps(6)
                        high(1)
                        if j == 1 and not first:
                            group_high(i)
                        exps(7)
                        exps(8)
                rounds(act, body)
                copy_pv(GROUPS - 1, 2, 1)
                copy_pv(GROUPS - 1, 3, 0)
                copy_pv(GROUPS - 1, 3, 1)
                group_high(GROUPS)
                group_out(GROUPS, 0)
                group_out(GROUPS, 1)

            @block.vector
            def _(dve):
                dve.wait_ge(s_const, 7)

                def seg_max(i, j, s):
                    n = 4 * i + j
                    t, k0, w, diagonal = SEGMENTS[s]
                    wait(dve, s_a, NSEG * n + s + 1)
                    src = a_bank[s % 3][:, 0:w]
                    nc.vector.tensor_reduce(mx[:, k0 // 512, t:t + 1], src, AX.X, ALU.max).then_inc(s_max, 1)

                def row_maxima(i, j):
                    n = 4 * i + j
                    wait(dve, s_max, NSEG * (n + 1))
                    nc.vector.tensor_tensor(row_max[:], mx[:, 0], mx[:, 1], ALU.max).then_inc(s_mc, 1)

                def max_high(i, j):
                    n = 4 * i + j
                    wait(dve, s_mc, 2 * n + 1)
                    wait(dve, s_mt, n)
                    nc.vector.tensor_scalar(m_row[:, 0:QT], row_max[:], -MAX_SCALE, None, ALU.mult).then_inc(s_mc, 1)

                def max_low(i, j):
                    n = 4 * i + j
                    wait(dve, s_mc, 2 * n + 2)
                    nc.vector.scalar_tensor_tensor(m_row[:, QT:2 * QT], row_max[:], -MAX_SCALE, m_row[:, 0:QT],
                                                   ALU.mult, ALU.subtract).then_inc(s_mr, 1)

                def high(i, j):
                    n = 4 * i + j
                    wait(dve, s_exp, UNITS * (n + 1))
                    nc.vector.tensor_copy(p_h[:, j % 2, 2 * CW:], p32[:, 2 * CW:]).then_inc(s_hid, 1)

                def low(i, j, c):
                    n = 4 * i + j
                    cs = slice(c * CW, (c + 1) * CW - POOL_W)
                    if c < 2:
                        wait(dve, s_hi, 2 * n + c + 1)
                    else:
                        wait(dve, s_hid, n + 1)
                    nc.vector.tensor_tensor(p_l[:, j % 2, cs], p32[:, cs], p_h[:, j % 2, cs], ALU.subtract).then_inc(s_lo, 1)

                def sum_parts(i, j):
                    wait(dve, s_c, 2 * (4 * i + j) + 2)
                    nc.vector.reciprocal(rsum[:], c32[:, :, 2 * HD])
                    nc.vector.tensor_tensor(osum[:], c32[:, :, 0:HD], c32[:, :, HD:2 * HD], ALU.add).then_inc(s_nc, 1)

                def normalise(i, j):
                    if j % 4 == 0:
                        wait(dve, s_ol, i + j // 4)
                    wait(dve, s_nc, 4 * i + j + 1)
                    nc.vector.tensor_tensor(o32[:, :, j % 4, :], osum[:], rsum[:].unsqueeze(2).to_broadcast([P, QT, HD]),
                                            ALU.mult).then_inc(s_norm, 1)

                def ffn_add(i, hf):
                    cs = slice(512 * hf, 512 * hf + 512)
                    wait(dve, s_f, 2 * i + hf + 1)
                    wait(dve, s_xf[hf], 16 * (i + 1))
                    wait(dve, s_yw[hf], 16 * i)
                    nc.vector.scalar_tensor_tensor(y_st[:, cs], ffn_bank[:], ffn_scale[:], xf[:, cs],
                                                   ALU.mult, ALU.add).then_inc(s_fe, 1)

                for j in range(2):
                    for s in range(NSEG):
                        seg_max(0, j, s)
                    row_maxima(0, j)
                    if j == 0:
                        max_high(0, j)
                        max_low(0, j)

                def body(i, first, last):
                    for j in range(4):
                        ahead = not (last and j >= 2)
                        behind = not (first and j == 0)

                        def maxima(s0, s1):
                            if ahead:
                                for s in range(s0, s1):
                                    seg_max(i, j + 2, s)

                        if not (last and j == 3):
                            max_high(i, j + 1)
                        maxima(0, 1)
                        if not (last and j == 3):
                            max_low(i, j + 1)
                        maxima(1, 3)
                        if behind:
                            high(i, j - 1)
                            low(i, j - 1, 2)
                        maxima(3, 4)
                        if not (first and j <= 1):
                            sum_parts(i, j - 2)
                        maxima(4, 5)
                        if not (first and j <= 1):
                            normalise(i, j - 2)
                        maxima(5, 7)
                        low(i, j, 0)
                        maxima(7, 11)
                        if j % 2 == 1:
                            ffn_add(i, j // 2)
                        maxima(11, NSEG)
                        if ahead:
                            row_maxima(i, j + 2)
                        low(i, j, 1)
                rounds(dve, body)
                high(GROUPS - 1, 3)
                low(GROUPS - 1, 3, 2)
                for j in (2, 3):
                    sum_parts(GROUPS - 1, j)
                    normalise(GROUPS - 1, j)

            @block.tensor
            def _(pe):
                pe.wait_ge(s_const, 7)

                def segment(i, j, s):
                    n, k = 4 * i + j, j % 4
                    t, k0, w, diagonal = SEGMENTS[s]
                    if s == 0:
                        wait(pe, s_ld[k], 64 * (i + j // 4 + 1))
                    wait(pe, s_max, NSEG * n + s - 2)
                    ins = pe.matmul(a_bank[s % 3][:, 0:w], q_st[0:KR, k, t * P:(t + 1) * P], k_st[0:KR, k, k0:k0 + w],
                                    start=True, stop=not diagonal)
                    if diagonal:
                        ins = pe.matmul(a_bank[s % 3][:, w - P:w], neg_id[:], past[:, 0], start=False, stop=True)
                    ins.then_inc(s_a, 1)

                def unit(i, j, u):
                    n, k = 4 * i + j, j % 4
                    if u == 0:
                        wait(pe, s_mrow[k], 32 * (i + 1))
                    wait(pe, s_exp, UNITS * n + u - 2)
                    acc = b_bank[u % 3]
                    for col, kt, t, tiles in unit_runs(u):
                        diagonal = t == kt
                        ins = pe.matmul(acc[:, col:col + tiles * P], k_st[0:KR + 2, k, kt * P:(kt + 1) * P],
                                        q_st[0:KR + 2, k, t * P:(t + tiles) * P], start=True, stop=not diagonal)
                        if diagonal:
                            ins = pe.matmul(acc[:, col:col + P], neg_id[:], past[:, 1], start=False, stop=True)
                    ins.then_inc(s_b, 1)

                def pv(i, j, t, turn_before):
                    n, k = 4 * i + j, j % 4
                    if t in (0, 3):
                        chunks = CHUNKS * n + (2 if t == 0 else 3)
                        if t == 0:
                            wait(pe, s_hi, 2 * n + 2)
                        else:
                            wait(pe, s_hid, n + 1)
                        wait(pe, s_lo, chunks)
                        wait(pe, s_lop, chunks)
                    if t == 0:
                        wait(pe, *turn_before)
                        wait(pe, s_ldv[k], 16 * (i + j // 4 + 1))
                    if t == 4:
                        wait(pe, s_c, 2 * n + 1)
                    acc = turn_bank[:, (t % 4) * VW:(t % 4 + 1) * VW]
                    for kt in range(t + 1):
                        at = SLOT[(kt, t)] * P
                        v = v_st[:, k, kt // 4, (kt % 4) * VW:(kt % 4 + 1) * VW]
                        pe.matmul(acc, p_h[:, j % 2, at:at + P], v, start=(kt == 0), stop=False)
                        ins = pe.matmul(acc, p_l[:, j % 2, at:at + P], v, start=False, stop=(kt == t))
                    ins.then_inc(s_pv, 1)

                def transpose_max(i, j, turn_before=None):
                    wait(pe, s_mr, 4 * i + j + 1)
                    if turn_before is not None:
                        wait(pe, *turn_before)
                    pe.transpose(turn_bank[0:2 * QT].bitcast(F16)[:, 0:P], m_row[:], ident[:]).then_inc(s_mt, 1)

                def transpose_group(i, part, turn_sem, turn):
                    src = (o_h, o_l)[part]
                    wait(pe, (s_oh, s_ol)[part], i)
                    wait(pe, turn_sem, turn)
                    for t in range(QT):
                        ins = pe.transpose(turn_bank[:].bitcast(F16)[:, t * P:(t + 1) * P], src[:, t * P:(t + 1) * P], ident[:])
                    ins.then_inc(s_ot, 1)

                def ffn(i, j):
                    hf = j // 2
                    if j % 2 == 0:
                        wait(pe, s_fe, 2 * i + hf)
                    for c in range(4 * (j % 2), 4 * (j % 2) + 4):
                        at = bass.ds(i * P, P)
                        cs = slice(512 * hf, 512 * hf + 512)
                        pe.matmul(ffn_bank[:], xnT_h[:, c, at], wfT_h[:, c, cs], start=(c == 0), stop=False)
                        pe.matmul(ffn_bank[:], xnT_h[:, c, at], wfT_l[:, c, cs], start=False, stop=False)
                        ins = pe.matmul(ffn_bank[:], xnT_l[:, c, at], wfT_h[:, c, cs], start=False, stop=(c == IC - 1))
                        yield
                    if j % 2 == 1:
                        ins.then_inc(s_f, 1)
                    yield

                for j in range(2):
                    for s in range(NSEG):
                        segment(0, j, s)
                    if j == 0:
                        transpose_max(0, 0)

                def body(i, first, last):
                    for j in range(4):
                        n = 4 * i + j
                        ahead = not (last and j >= 2)
                        behind = not (first and j == 0)
                        turn = (s_mcp, n + 1) if first and j <= 1 else (s_c, 2 * (n - 1))
                        filler = ffn(i, j)
                        for u in range(UNITS):
                            unit(i, j, u)
                            if ahead:
                                for s in SEGMENTS_AFTER_UNIT[u]:
                                    segment(i, j + 2, s)
                            if u % 2 == 1:
                                next(filler)
                            if u == 2 and not (last and j == 3):
                                transpose_max(i, j + 1, turn)
                                turn = (s_mcp, n + 2)
                            if u == 4 and j in (2, 3) and not first:
                                transpose_group(i, j - 2, *turn)
                                turn = ((s_oth, s_otl)[j - 2], i)
                            if behind:
                                for t in {5: (0, 1, 2, 3), 7: (4, 5), 8: (6, 7)}.get(u, ()):
                                    pv(i, j - 1, t, turn)
                        next(filler)
                rounds(pe, body)
                for t in range(QT):
                    pv(GROUPS - 1, 3, t, (s_c, 2 * (PAIRS - 1)))
                transpose_group(GROUPS, 0, s_c, 2 * PAIRS)
                transpose_group(GROUPS, 1, s_oth, GROUPS)

    step5 = ExitStack()
    with step5:
        wo_raw = sb(step5, "wo_raw", [P, IC, D], F32)
        wo_h = sb(step5, "wo_h", [P, IC, D], F16)
        wo_l = sb(step5, "wo_l", [P, IC, D], F16)
        y_in = sb(step5, "y_in", [P, 2, D], F32)
        y_out = sb(step5, "y_out", [P, 2, D], F32)
        oT = (xnT_h, xnT_l)
        s_wo = [sem(f"wo_loaded{c}") for c in range(4)]
        s_oT = [sem(f"oT_loaded{c}") for c in range(4)]
        s_woh = sem("wo_high_ready")
        s_wol = sem("wo_low_ready")
        s_y = [sem(f"y_loaded{k}") for k in range(2)]
        s_op = sem("out_product_ready")
        s_add = sem("out_added")
        s_out = [sem(f"out_written{k}") for k in range(2)]
        with nc.Block("project") as block:
            @block.sync
            def _(sp):
                view = wo.rearrange("(c p) n -> p c n", p=P)
                for c in range(4):
                    sp.dma_start(wo_raw[:, 2 * c:2 * c + 2, :], view[:, 2 * c:2 * c + 2, :]).then_inc(s_wo[c], 16)
                for c in range(4):
                    for r in range(2):
                        src = o_scr[IC * (c // 2):IC * (c // 2 + 1), :, r, 512 * (c % 2):512 * (c % 2) + 512]
                        sp.dma_start(oT[r][:, :, 512 * c:512 * c + 512], src.rearrange("c p s -> p c s")).then_inc(s_oT[c], 16)
                for k in range(2):
                    sp.dma_start(y_in[:, k], y_scr[k]).then_inc(s_y[k], 16)

                def body(i, last):
                    for k in range(2):
                        t = held(sp, 2 * i + k)
                        ahead = held(sp, t + 2)
                        wait(sp, s_add, 2 * t + 2)
                        sp.dma_start(out_tiles[bass.ds(t, 1)].rearrange("a p d -> (a p) d"), y_out[:, k]).then_inc(s_out[k], 16)
                        if not last:
                            sp.dma_start(y_in[:, k], y_scr[bass.ds(ahead, 1)].rearrange("a p d -> (a p) d")).then_inc(s_y[k], 16)
                with sp.Fori(0, TT // 2 - 1) as i:
                    body(i, False)
                body(TT // 2 - 1, True)
                for k in range(2):
                    sp.wait_ge(s_out[k], 16 * TT // 2)

            @block.scalar
            def _(act):
                for c in range(IC):
                    act.wait_ge(s_wo[c // 2], 16)
                    act.activation(wo_h[:, c, :], wo_raw[:, c, :], ACT.Copy, scale=w_up[:, 3:4]).then_inc(s_woh, 1)

            @block.vector
            def _(dve):
                for c in range(IC):
                    dve.wait_ge(s_woh, c + 1)
                    nc.vector.scalar_tensor_tensor(wo_l[:, c, :], wo_raw[:, c, :], w_up[:, 3:4], wo_h[:, c, :],
                                                   ALU.mult, ALU.subtract).then_inc(s_wol, 1)

                def body(i, first):
                    for k in range(2):
                        t = 2 * i + k
                        for n in range(2):
                            cs = slice(512 * n, 512 * n + 512)
                            wait(dve, s_op, 2 * t + n + 1)
                            if n == 0:
                                wait(dve, s_y[k], 16 * (i + 1))
                                if not first:
                                    wait(dve, s_out[k], 16 * i)
                            nc.vector.scalar_tensor_tensor(y_out[:, k, cs], banks[2 * k + n][:], attn_scale[:],
                                                           y_in[:, k, cs], ALU.mult, ALU.add).then_inc(s_add, 1)
                body(0, True)
                with dve.Fori(1, TT // 2) as i:
                    body(i, False)

            @block.tensor
            def _(pe):
                pe.wait_ge(s_woh, IC)
                pe.wait_ge(s_wol, IC)
                for c in range(4):
                    pe.wait_ge(s_oT[c], 32)

                def body(i, first):
                    for k in range(2):
                        t = 2 * i + k
                        for n in range(2):
                            if not first:
                                wait(pe, s_add, 2 * (t - 2) + n + 1)
                            acc = banks[2 * k + n]
                            cs = slice(512 * n, 512 * n + 512)
                            at = bass.ds(t * P, P)
                            for c in range(IC):
                                pe.matmul(acc[:], oT[0][:, c, at], wo_h[:, c, cs], start=(c == 0), stop=False)
                                pe.matmul(acc[:], oT[0][:, c, at], wo_l[:, c, cs], start=False, stop=False)
                                ins = pe.matmul(acc[:], oT[1][:, c, at], wo_h[:, c, cs], start=False, stop=(c == IC - 1))
                            ins.then_inc(s_op, 1)
                body(0, True)
                with pe.Fori(1, TT // 2) as i:
                    body(i, False)


_INS = ["L0_attn_x", "L0_attn_wq", "L0_attn_wk", "L0_attn_wv", "L0_attn_wo", "L0_ffn_W_q", "L0_ffn_scale", "L0_ffn_zero"]


def kernel(**inputs):
    import numpy as _np
    import concourse.bacc as _bacc
    from concourse import mybir as _mybir
    from concourse.bass_utils import run_bass_kernel_spmd as _run

    nc = _bacc.Bacc("TRN2", target_bir_lowering=False, num_devices=1)
    arrays, args = {}, []

    def give(name, a):
        a = _np.ascontiguousarray(a)
        arrays[name] = a
        args.append(nc.dram_tensor(name, a.shape, _mybir.dt.from_np(a.dtype), kind="ExternalInput").ap())

    for name in _INS:
        give(f"in_{name}", inputs[name])
    inv = 1.0 / 10000.0 ** (_np.arange(0, HD, 2)[:HD // 2].astype(_np.float32) / HD)
    angle = _np.outer(_np.arange(S), inv).astype(_np.float32)
    for name, f in (("cos_table", _np.cos), ("sin_table", _np.sin)):
        give(name, _np.tile(f(angle).T * _np.float32(QK_SCALE), (P // (HD // 2), 1)).astype(_np.float32))
    args.append(nc.dram_tensor("out_0_dram", (B, S, D), F32, kind="ExternalOutput").ap())
    build(nc, *args)
    r = _run(nc, [arrays], core_ids=[0])
    return r.results[0]["out_0_dram"]
```

```python
from contextlib import ExitStack

import concourse.bass as bass
from concourse import mybir

F32 = mybir.dt.float32
F16 = mybir.dt.float16
I32 = mybir.dt.int32
ALU = mybir.AluOpType
ACT = mybir.ActivationFunctionType
AX = mybir.AxisListType
RMAX = bass.bass_isa.ReduceOp.max

P = 128
B, S, D = 2, 1024, 1024
H, HD = 32, 32
TOK = B * S
IC = D // P
TT = TOK // P
QT = S // P
PAIRS = B * H
GROUP = 64
NG = D // GROUP
VW = 2 * HD + 1
EPS = 1e-5

XN_SCALE = 2.0 ** 10
W_TOP = 2.0 ** 14
QK_SCALE = 2.0 ** -23
V_SCALE = 2.0 ** -20
MAX_SCALE = 2.0 ** -15
MASKED = 2.0 ** 60

KEY_ORDER = [0, 1, 7, 2, 6, 3, 5, 4]
BLOCKS = [(j, t) for j in KEY_ORDER for t in range(j, QT)]
SLOT = {jt: n for n, jt in enumerate(BLOCKS)}
UNIT = 4
UNITS = len(BLOCKS) // UNIT
CHUNK = 3
CHUNKS = UNITS // CHUNK
CW = CHUNK * UNIT * P
SEGMENTS = [(t, 0, 512, False) for t in range(4, QT)] + \
           [(t, 0, (t + 1) * P, True) for t in range(4)] + \
           [(t, 512, (t - 3) * P, True) for t in range(4, QT)]
NSEG = len(SEGMENTS)
SEGMENTS_AFTER_UNIT = [(0, 1), (2,), (3,), (4, 5), (6,), (7,), (8, 9), (10,), (11,)]


def unit_runs(u):
    runs = []
    for k in range(UNIT):
        j, t = BLOCKS[u * UNIT + k]
        if runs and runs[-1][1] == j:
            runs[-1][3] += 1
        else:
            runs.append([k * P, j, t, 1])
    return runs


def wait(eng, sem, value):
    if isinstance(value, int) and value <= 0:
        return
    eng.wait_ge(sem, value)


def held(eng, value):
    return value if isinstance(value, int) else eng.snap(value)


def build(nc, x, wq, wk, wv, wo, w_packed, w_scale, w_zero, cos_t, sin_t, out):
    q_scr = nc.dram_tensor("q_scr", (B, H, 2, HD, S), F16, kind="Internal").ap()
    k_scr = nc.dram_tensor("k_scr", (B, H, 2, HD, S), F16, kind="Internal").ap()
    v_scr = nc.dram_tensor("v_scr", (B, H, 2, P, 4 * VW), F16, kind="Internal").ap()
    y_scr = nc.dram_tensor("y_scr", (TT, P, D), F32, kind="Internal").ap()
    o_scr = nc.dram_tensor("o_scr", (B * IC, P, 2, S), F16, kind="Internal").ap()
    x_tiles = x.rearrange("b (t p) d -> (b t) p d", p=P)
    out_tiles = out.rearrange("b (t p) d -> (b t) p d", p=P)

    with ExitStack() as whole:
        def sb(ctx, name, shape, dt):
            return ctx.enter_context(nc.sbuf_tensor(name, shape, dt))

        def sem(name):
            return whole.enter_context(nc.semaphore(name))

        banks = [whole.enter_context(nc.psum_tensor(f"bank{i}", [P, 512], F32)) for i in range(8)]
        ident = sb(whole, "ident", [P, P], F16)
        w_absmax = sb(whole, "w_absmax", [P, 5], F32)
        w_pow2 = sb(whole, "w_pow2", [P, 5], F32)
        w_up = sb(whole, "w_up", [P, 5], F32)
        w_down = sb(whole, "w_down", [P, 5], F32)
        exp_scale = sb(whole, "exp_scale", [P, 1], F32)
        attn_scale = sb(whole, "attn_scale", [P, 1], F32)
        ffn_scale = sb(whole, "ffn_scale", [P, 1], F32)
        xnT_h = sb(whole, "xnT_h", [P, IC, TOK], F16)
        xnT_l = sb(whole, "xnT_l", [P, IC, TOK], F16)

        def pow2_scales(dve, chain, c0, c1):
            cs = slice(c0, c1)
            chain(nc.vector.tensor_scalar(w_pow2[:, cs], w_absmax[:, cs], 1e-30, None, ALU.max))
            chain(nc.vector.tensor_scalar(w_pow2[:, cs].bitcast(I32), w_pow2[:, cs].bitcast(I32),
                                          0x7F800000, None, ALU.bitwise_and))
            chain(nc.vector.reciprocal(w_up[:, cs], w_pow2[:, cs]))
            chain(nc.vector.tensor_scalar(w_up[:, cs], w_up[:, cs], W_TOP, None, ALU.mult))
            chain(nc.vector.tensor_scalar(w_down[:, cs], w_pow2[:, cs], 1.0 / W_TOP, None, ALU.mult))

        w_raw = sb(whole, "w_raw", [P, IC, D], F32)
        wfT = w_raw[:].rearrange("p c d -> p (c d)").bitcast(F16).rearrange("p (r c d) -> p r c d", r=2, c=IC)
        wfT_h, wfT_l = wfT[:, 0], wfT[:, 1]
        qk_raw = w_raw[:, 0:4, :].rearrange("p a b -> p (a b)").rearrange("p (w c n) -> p w c n", w=2, c=IC)
        cosb, sinb = w_raw[:, 4, :], w_raw[:, 5, :]
        qk_views = [w.rearrange("(c p) n -> p c n", p=P) for w in (wq, wk)]
        s_raw = [sem(f"qk_weight_loaded{k}") for k in range(2)]
        s_tab = sem("tables_loaded")

        step1 = ExitStack()
        with step1:
            GT = 4
            wv_h = sb(step1, "wv_h", [P, IC, D], F16)
            wv_l = sb(step1, "wv_l", [P, IC, D], F16)
            xt = sb(step1, "xt", [P, 2, GT, D], F32)
            xh = sb(step1, "xh", [P, 2, D], F16)
            xl = sb(step1, "xl", [P, 2, D], F16)
            stats = sb(step1, "stats", [P, GT, 2, 6], F32)
            mv = sb(step1, "mv", [P, GT, 2], F32)
            sd = sb(step1, "sd", [P, GT], F32)
            ve = sb(step1, "ve", [P, GT], F32)
            rstd = sb(step1, "rstd", [P, GT], F32)
            tmp = sb(step1, "tmp", [P, GT], F32)
            shift = sb(step1, "shift", [P, GT], F32)
            v_st = sb(step1, "v_st", [P, 2, H, GT * VW], F16)
            wmx = sb(step1, "wmx", [P, 16], F32)

            s_id = sem("ident_ready")
            s_wv = [sem(f"wv_loaded{c}") for c in range(4)]
            s_bg = [sem(f"weight_loaded{c}") for c in range(4)]
            s_x = [sem(f"x_loaded{k}") for k in range(2)]
            s_chain = sem("dve_small_done")
            s_wmax = sem("wv_max_ready")
            s_wall = sem("wv_max_all_ready")
            s_wup = sem("wv_scale_ready")
            s_wh = sem("wv_high_ready")
            s_wl = sem("wv_low_ready")
            s_var = sem("variance_ready")
            s_sd = sem("deviation_ready")
            s_rs = sem("rstd_ready")
            s_xn = sem("xn_ready")
            s_xh = sem("xn_high_ready")
            s_xl = sem("xn_low_ready")
            s_tr = sem("xn_transposed")
            s_th = sem("xnT_high_stored")
            s_tl = sem("xnT_low_stored")
            s_v = sem("v_product_ready")
            s_vh = sem("v_high_ready")
            s_vl = sem("v_low_ready")
            s_vw = [sem(f"v_written{k}") for k in range(2)]
            s_bgm = sem("weight_slab_reduced")
            s_all4 = sem("weight_max_all_ready")
            NT1 = TT // GT
            slabs = [(w, c) for w in (wq, wk, wo) for c in range(4)]
            slab_view = [w.rearrange("(c p) n -> p c n", p=P)[:, 2 * c:2 * c + 2, :] for w, c in slabs]

            with nc.Block("norm_v") as block:
                @block.sync
                def _(sp):
                    wv_view = wv.rearrange("(c p) n -> p c n", p=P)
                    def load_x(it):
                        sp.dma_start(xt[:, it % 2], x_tiles[GT * it:GT * it + GT].rearrange("t p d -> p t d")).then_inc(s_x[it % 2], 16)

                    load_x(0)
                    for c in range(4):
                        sp.dma_start(w_raw[:, 2 * c:2 * c + 2, :], wv_view[:, 2 * c:2 * c + 2, :]).then_inc(s_wv[c], 16)
                    load_x(1)
                    wait(sp, s_wh, IC)
                    wait(sp, s_wl, IC)
                    for n in range(12):
                        if n >= 4:
                            wait(sp, s_bgm, n - 3)
                        sp.dma_start(w_raw[:, 2 * (n % 4):2 * (n % 4) + 2, :], slab_view[n]).then_inc(s_bg[n % 4], 16)
                        if n % 6 == 5:
                            it = n // 6
                            wait(sp, s_xl, GT * (it + 1))
                            load_x(it + 2)
                    for w in range(2):
                        wait(sp, s_bgm, 9 + w)
                        sp.dma_start(qk_raw[:, w], qk_views[w][:, :, 0:256]).then_inc(s_raw[w], 16)
                    wait(sp, s_bgm, 11)
                    sp.dma_start(cosb, cos_t).then_inc(s_tab, 16)
                    sp.dma_start(sinb, sin_t).then_inc(s_tab, 16)

                @block.gpsimd
                def _(pool):
                    pool.memset(ident[:], 0.0).then_inc(s_id, 1)
                    pool.wait_ge(s_id, 1)
                    pool.affine_select(out=ident[:], in_=ident[:], compare_op=ALU.not_equal, fill=1.0, base=0,
                                       pattern=[[-1, P]], channel_multiplier=1).then_inc(s_id, 1)
                    for k in range(2):
                        for h in range(GT):
                            pool.memset(v_st[:, k, :, (h + 1) * VW - 1:(h + 1) * VW], 1.0).then_inc(s_id, 1)
                    pool.wait_ge(s_wmax, 1)
                    pool.partition_all_reduce(w_absmax[:, 2:3], wmx[:, 4:5], P, RMAX).then_inc(s_wall, 1)
                    for it in range(NT1):
                        if it == NT1 - 1:
                            pool.wait_ge(s_bgm, 13)
                            pool.partition_all_reduce(wmx[:, 13:16], wmx[:, 13:16], P, RMAX).then_inc(s_all4, 1)
                        wait(pool, s_vh, 8 * (it + 1))
                        wait(pool, s_vl, 8 * (it + 1))
                        if it == 0:
                            pool.wait_ge(s_id, 2 + 2 * GT)
                        pool.dma_start(v_scr[it // 2, :, it % 2].rearrange("h p c -> p h c"), v_st[:, it % 2]).then_inc(s_vw[it % 2], 16)
                    for k in range(2):
                        wait(pool, s_vw[k], 32)

                @block.scalar
                def _(act):
                    def v_high(t):
                        for n in range(2):
                            wait(act, s_v, 2 * t + n + 1)
                            k, r = (t // GT) % 2, t % GT
                            if t >= 2 * GT and n == 0 and r == 0:
                                wait(act, s_vw[k], 16)
                            act.activation(v_st[:, k, 16 * n:16 * n + 16, r * VW:r * VW + HD],
                                           banks[4 + 2 * (t % 2) + n][:].rearrange("p (h d) -> p h d", d=HD),
                                           ACT.Copy, scale=V_SCALE).then_inc(s_vh, 1)

                    def x_high(t):
                        it, r = t // GT, t % GT
                        if r == 0:
                            act.wait_ge(s_var, it + 1)
                            act.activation(sd[:], ve[:], ACT.Sqrt).then_inc(s_sd, 1)
                            act.wait_ge(s_rs, it + 1)
                        wait(act, s_tr, 2 * (t - 2) + 1)
                        wait(act, s_xl, t - 1)
                        act.activation(xh[:, t % 2], xt[:, it % 2, r], ACT.Identity, bias=shift[:, r:r + 1],
                                       scale=rstd[:, r:r + 1]).then_inc(s_xh, 1)

                    x_high(0)
                    x_high(1)
                    act.wait_ge(s_wup, 1)
                    for c in range(IC):
                        act.activation(wv_h[:, c, :], w_raw[:, c, :], ACT.Copy, scale=w_up[:, 2:3]).then_inc(s_wh, 1)
                    for t in range(TT):
                        act.wait_ge(s_tr, 2 * t + 1)
                        act.activation(xnT_h[:, :, t * P:(t + 1) * P],
                                       banks[0 + 2 * (t % 2)][:].bitcast(F16).rearrange("p (c s) -> p c s", s=P),
                                       ACT.Copy).then_inc(s_th, 1)
                        if t + 2 < TT:
                            x_high(t + 2)
                        if t >= 1:
                            v_high(t - 1)
                    v_high(TT - 1)

                @block.vector
                def _(dve):
                    done = [0]

                    def chain(ins):
                        done[0] += 1
                        ins.then_inc(s_chain, 1)
                        dve.wait_ge(s_chain, done[0])

                    def split_wv():
                        dve.wait_ge(s_wall, 1)
                        pow2_scales(dve, chain, 2, 3)
                        chain(nc.vector.tensor_copy(tmp[:, 0:1], w_up[:, 2:3]))
                        nc.vector.tensor_copy(tmp[:, 1:2], w_up[:, 2:3]).then_inc(s_wup, 1)
                        for c in range(IC):
                            dve.wait_ge(s_wh, c + 1)
                            nc.vector.scalar_tensor_tensor(wv_l[:, c, :], w_raw[:, c, :], w_up[:, 2:3], wv_h[:, c, :],
                                                           ALU.mult, ALU.subtract).then_inc(s_wl, 1)

                    def v_low(t):
                        for n in range(2):
                            dve.wait_ge(s_vh, 2 * t + n + 1)
                            k, r = (t // GT) % 2, t % GT
                            nc.vector.scalar_tensor_tensor(
                                v_st[:, k, 16 * n:16 * n + 16, r * VW + HD:r * VW + 2 * HD],
                                banks[4 + 2 * (t % 2) + n][:].rearrange("p (h d) -> p h d", d=HD), V_SCALE,
                                v_st[:, k, 16 * n:16 * n + 16, r * VW:r * VW + HD],
                                ALU.mult, ALU.subtract).then_inc(s_vl, 1)

                    slab = [0]

                    def slab_max():
                        n = slab[0]
                        if n < 12:
                            slab[0] += 1
                            dve.wait_ge(s_bg[n % 4], 16 * (n // 4 + 1))
                            nc.vector.tensor_reduce(wmx[:, n:n + 1], w_raw[:, 2 * (n % 4):2 * (n % 4) + 2, :], AX.XY,
                                                    ALU.max, apply_absolute_value=True).then_inc(s_bgm, 1)

                    def statistics(it):
                        dve.wait_ge(s_x[it % 2], 16 * (it // 2 + 1))
                        for r in range(GT):
                            for k in range(2):
                                ins = nc.vector.bn_stats(stats[:, r, k, :], xt[:, it % 2, r, 512 * k:512 * k + 512])
                        chain(ins)
                        for r in range(GT):
                            ins = nc.vector.bn_aggr(mv[:, r, :], stats[:, r, :, :].rearrange("p a b -> p (a b)"))
                        chain(ins)
                        nc.vector.tensor_scalar(ve[:], mv[:, :, 1], EPS, None, ALU.add).then_inc(s_var, 1)
                        dve.wait_ge(s_var, it + 1)
                        dve.wait_ge(s_sd, it + 1)
                        chain(nc.vector.reciprocal(rstd[:], sd[:]))
                        chain(nc.vector.tensor_tensor(tmp[:], ve[:], rstd[:], ALU.mult))
                        chain(nc.vector.tensor_tensor(tmp[:], tmp[:], rstd[:], ALU.mult))
                        chain(nc.vector.tensor_scalar(tmp[:], tmp[:], -0.5, 1.5, ALU.mult, ALU.add))
                        chain(nc.vector.tensor_scalar(tmp[:], tmp[:], XN_SCALE, None, ALU.mult))
                        chain(nc.vector.tensor_tensor(rstd[:], rstd[:], tmp[:], ALU.mult))
                        chain(nc.vector.tensor_tensor(tmp[:], mv[:, :, 0], rstd[:], ALU.mult))
                        nc.vector.tensor_scalar(shift[:], tmp[:], -1.0, None, ALU.mult).then_inc(s_rs, 1)
                        dve.wait_ge(s_rs, it + 1)

                    def x_low(t):
                        it, r = t // GT, t % GT
                        dve.wait_ge(s_xh, t + 1)
                        chain(nc.vector.tensor_scalar(xt[:, it % 2, r], xt[:, it % 2, r], rstd[:, r:r + 1],
                                                      shift[:, r:r + 1], ALU.mult, ALU.add))
                        wait(dve, s_tr, 2 * (t - 1))
                        nc.vector.tensor_tensor(xl[:, t % 2], xt[:, it % 2, r], xh[:, t % 2],
                                                ALU.subtract).then_inc(s_xl, 1)

                    def weight_maxima():
                        dve.wait_ge(s_bgm, 12)
                        for w in range(3):
                            ins = nc.vector.tensor_reduce(wmx[:, 13 + w:14 + w], wmx[:, 4 * w:4 * w + 4], AX.X, ALU.max)
                        ins.then_inc(s_bgm, 1)

                    def weight_scales():
                        dve.wait_ge(s_all4, 1)
                        for src, dst in ((13, 0), (14, 1), (15, 3)):
                            chain(nc.vector.tensor_copy(w_absmax[:, dst:dst + 1], wmx[:, src:src + 1]))
                        pow2_scales(dve, chain, 0, 2)
                        pow2_scales(dve, chain, 3, 4)
                        chain(nc.vector.tensor_tensor(exp_scale[:], w_down[:, 0:1], w_down[:, 1:2], ALU.mult))
                        chain(nc.vector.tensor_scalar(exp_scale[:], exp_scale[:], 1.0 / (QK_SCALE * XN_SCALE) ** 2,
                                                      float(HD) ** -0.5, ALU.mult, ALU.mult))
                        chain(nc.vector.tensor_tensor(attn_scale[:], w_down[:, 2:3], w_down[:, 3:4], ALU.mult))
                        chain(nc.vector.tensor_scalar(attn_scale[:], attn_scale[:], 1.0 / (V_SCALE * XN_SCALE), None, ALU.mult))

                    statistics(0)
                    x_low(0)
                    x_low(1)
                    for c in range(4):
                        dve.wait_ge(s_wv[c], 16)
                        chain(nc.vector.tensor_reduce(wmx[:, c:c + 1], w_raw[:, 2 * c:2 * c + 2, :], AX.XY, ALU.max,
                                                      apply_absolute_value=True))
                    nc.vector.tensor_reduce(wmx[:, 4:5], wmx[:, 0:4], AX.X, ALU.max).then_inc(s_wmax, 1)
                    split_wv()
                    for t in range(TT):
                        dve.wait_ge(s_tr, 2 * t + 2)
                        nc.vector.tensor_copy(xnT_l[:, :, t * P:(t + 1) * P],
                                              banks[1 + 2 * (t % 2)][:].bitcast(F16).rearrange("p (c s) -> p c s", s=P)
                                              ).then_inc(s_tl, 1)
                        if t + 2 < TT:
                            if (t + 2) % GT == 0:
                                statistics((t + 2) // GT)
                            x_low(t + 2)
                        if t >= 1:
                            v_low(t - 1)
                        slab_max()
                        if t == 12:
                            weight_maxima()
                        if t == 13:
                            weight_scales()
                    v_low(TT - 1)

                @block.tensor
                def _(pe):
                    pe.wait_ge(s_id, 2)

                    def v_product(t):
                        pe.wait_ge(s_th, t + 1)
                        pe.wait_ge(s_tl, t + 1)
                        for n in range(2):
                            wait(pe, s_vl, 2 * (t - 2) + n + 1)
                            acc = banks[4 + 2 * (t % 2) + n]
                            cols = slice(512 * n, 512 * n + 512)
                            for c in range(IC):
                                if t == 0 and n == 0:
                                    pe.wait_ge(s_wh, c + 1)
                                    pe.wait_ge(s_wl, c + 1)
                                hi, lo = xnT_h[:, c, t * P:(t + 1) * P], xnT_l[:, c, t * P:(t + 1) * P]
                                pe.matmul(acc[:], hi, wv_h[:, c, cols], start=(c == 0), stop=False)
                                pe.matmul(acc[:], hi, wv_l[:, c, cols], start=False, stop=False)
                                ins = pe.matmul(acc[:], lo, wv_h[:, c, cols], start=False, stop=(c == IC - 1))
                            ins.then_inc(s_v, 1)

                    for t in range(TT):
                        for part, ready, read, bank in ((xh, s_xh, s_th, 0), (xl, s_xl, s_tl, 1)):
                            pe.wait_ge(ready, t + 1)
                            wait(pe, read, t - 1)
                            dst = banks[bank + 2 * (t % 2)][:].bitcast(F16)
                            for c in range(IC):
                                ins = pe.transpose(dst[:, c * P:(c + 1) * P], part[:, t % 2, c * P:(c + 1) * P], ident[:])
                            ins.then_inc(s_tr, 1)
                        if t >= 1:
                            v_product(t - 1)
                    v_product(TT - 1)

        step2 = ExitStack()
        unpacked = whole.enter_context(ExitStack())
        wf = sb(unpacked, "wf", [P, D // P, D], F32)
        with step2:
            HG = 8
            NGRP = H // HG
            raw = qk_raw
            wh = sb(step2, "qk_wh", [P, 2, IC, 2, P], F16)
            wl = sb(step2, "qk_wl", [P, 2, IC, 2, P], F16)
            packed = sb(step2, "packed", [P, 2, D // 2], I32)
            nib = sb(step2, "nib", [P, 2, D // 2], I32)
            zs = sb(step2, "zs", [P, 2, D // P, NG], F32)
            fmx = sb(step2, "fmx", [P, D // P + 1], F32)
            prod = sb(step2, "prod", [P, 2, 4, 512], F32)
            rot = sb(step2, "rot", [P, 2, 2, 512], F32)
            rh = sb(step2, "rh", [P, 2, 2, 512], F16)
            rl = sb(step2, "rl", [P, 2, 2, 512], F16)
            s_pk = [sem(f"packed_loaded{k}") for k in range(2)]
            s_zs = sem("zero_scale_loaded")
            s_nib = sem("nibbles_ready")
            s_fc = sem("ffn_small_done")
            s_fm = sem("ffn_max_ready")
            s_fa = sem("ffn_max_all_ready")
            s_qwh = sem("qk_weight_high")
            s_qwl = sem("qk_weight_low")
            s_ps = sem("qk_product_ready")
            s_pr = sem("rotation_products_ready")
            s_rot = sem("rotated_ready")
            s_rh = sem("rotated_high_ready")
            s_rl = sem("rotated_low_ready")
            s_st = [sem(f"qk_written{k}") for k in range(2)]
            TC = TOK // 512
            CH = 2 * TC

            with nc.Block("qk") as block:
                @block.sync
                def _(sp):
                    packed_tiles = w_packed.rearrange("(t p n) -> t p n", p=P, n=D // 2)
                    sp.dma_start(zs[:, 0], w_zero.rearrange("(t p g) -> p t g", p=P, g=NG)).then_inc(s_zs, 16)
                    sp.dma_start(zs[:, 1], w_scale.rearrange("(t p g) -> p t g", p=P, g=NG)).then_inc(s_zs, 16)
                    for r in range(2):
                        sp.dma_start(packed[:, r], packed_tiles[r]).then_inc(s_pk[r], 16)
                    with sp.Fori(1, NGRP) as g:
                        for w in range(2):
                            wait(sp, s_qwl, 2 * (g - 1) + w + 1)
                            sp.dma_start(raw[:, w], qk_views[w][:, :, bass.ds(g * 256, 256)]).then_inc(s_raw[w], 16)
                        for r in range(2):
                            wait(sp, s_nib, 2 * (g - 1) + r + 1)
                            sp.dma_start(packed[:, r], packed_tiles[bass.ds(2 * g + r, 1)].rearrange("a p n -> (a p) n")
                                         ).then_inc(s_pk[r], 16)

                def chunk_out(eng, g, w, tc, part, ab, src):
                    scr = q_scr if w == 0 else k_scr
                    dst = scr[tc // 2, :, part, 16 * ab:16 * ab + 16, 512 * (tc % 2):512 * (tc % 2) + 512]
                    return eng.dma_start(dst[bass.ds(g * HG, HG)].rearrange("h i s -> h i s"), src)

                @block.gpsimd
                def _(pool):
                    def group(g):
                        for w in range(2):
                            for tc in range(TC):
                                m = w * TC + tc
                                k = m % 2
                                n = g * CH + m
                                wait(pool, s_pr, n + 1)
                                if m >= 2 or not isinstance(g, int):
                                    wait(pool, s_rl, 2 * (n - 1))
                                nc.gpsimd.tensor_tensor(rot[:, k, 0], prod[:, k, 0], prod[:, k, 1], ALU.subtract).then_inc(s_rot, 1)
                                nc.gpsimd.tensor_tensor(rot[:, k, 1], prod[:, k, 2], prod[:, k, 3], ALU.add).then_inc(s_rot, 1)
                    group(0)
                    with pool.Fori(1, NGRP) as g:
                        group(g)
                    pool.wait_ge(s_fm, 1)
                    pool.partition_all_reduce(w_absmax[:, 4:5], fmx[:, D // P:D // P + 1], P, RMAX).then_inc(s_fa, 1)

                @block.scalar
                def _(act):
                    def split(g, w):
                        wait(act, s_raw[w], 16 * (g + 1))
                        wait(act, s_ps, (g - 1) * CH + (w + 1) * TC)
                        for ab in range(2):
                            act.activation(wh[:, w, :, ab, :], raw[:, w].rearrange("p c (m a) -> p a c m", a=2)[:, ab],
                                           ACT.Copy, scale=w_up[:, w:w + 1]).then_inc(s_qwh, 1)

                    def group(g, last=False):
                        first = isinstance(g, int) and g == 0
                        for w in range(2):
                            if w == 0:
                                split(g, 1)
                            elif not last:
                                split(g + 1, 0)
                            for tc in range(TC):
                                m = w * TC + tc
                                k = m % 2
                                n = g * CH + m
                                for ab in range(2):
                                    wait(act, s_rot, 2 * n + ab + 1)
                                    if ab == 0 and (m >= 2 or not first):
                                        wait(act, s_st[k], 64 * (g * (CH // 2) + m // 2))
                                    act.activation(rh[:, k, ab], rot[:, k, ab], ACT.Copy).then_inc(s_rh, 1)
                                wait(act, s_rl, 2 * (n + 1))
                                wait(act, s_rh, 2 * (n + 1))
                                for part, src in ((0, rh), (1, rl)):
                                    for ab in range(2):
                                        chunk_out(act, g, w, tc, part, ab, src[:, k, ab]).then_inc(s_st[k], 16)
                    split(0, 0)
                    group(0)
                    with act.Fori(1, NGRP - 1) as g:
                        group(g)
                    group(NGRP - 1, last=True)
                    for k in range(2):
                        act.wait_ge(s_st[k], 64 * NGRP * CH // 2)

                @block.vector
                def _(dve):
                    def split(g, w):
                        for ab in range(2):
                            wait(dve, s_qwh, 4 * g + 2 * w + ab + 1)
                            for c4 in range(2):
                                cs = slice(4 * c4, 4 * c4 + 4)
                                ins = nc.vector.scalar_tensor_tensor(
                                    wl[:, w, cs, ab, :], raw[:, w, cs].rearrange("p c (m a) -> p a c m", a=2)[:, ab],
                                    w_up[:, w:w + 1], wh[:, w, cs, ab, :], ALU.mult, ALU.subtract)
                        ins.then_inc(s_qwl, 1)

                    def group(g, last=False):
                        first = isinstance(g, int) and g == 0
                        if first:
                            dve.wait_ge(s_tab, 32)

                        def rotate(m):
                            k = m % 2
                            n = g * CH + m
                            wait(dve, s_ps, n + 1)
                            if m >= 2 or not first:
                                wait(dve, s_rot, 2 * (n - 1))
                            s0 = 512 * (m % 2)
                            c, s = cosb[:, s0:s0 + 512], sinb[:, s0:s0 + 512]
                            even, odd = banks[2 * k][:], banks[2 * k + 1][:]
                            nc.vector.tensor_tensor(prod[:, k, 0], even, c, ALU.mult)
                            nc.vector.tensor_tensor(prod[:, k, 1], odd, s, ALU.mult)
                            nc.vector.tensor_tensor(prod[:, k, 2], even, s, ALU.mult)
                            nc.vector.tensor_tensor(prod[:, k, 3], odd, c, ALU.mult).then_inc(s_pr, 1)

                        def low(m):
                            k = m % 2
                            n = g * CH + m
                            for ab in range(2):
                                wait(dve, s_rh, 2 * n + ab + 1)
                                nc.vector.tensor_tensor(rl[:, k, ab], rot[:, k, ab], rh[:, k, ab],
                                                        ALU.subtract).then_inc(s_rl, 1)

                        def unpack(g, r):
                            t = 2 * g + r
                            one = bass.ds(t, 1)
                            if first and r == 0:
                                dve.wait_ge(s_zs, 32)
                            wait(dve, s_pk[r], 16 * (g + 1))
                            nc.vector.tensor_scalar(nib[:, 0], packed[:, r], 15, None, ALU.bitwise_and)
                            nc.vector.tensor_scalar(nib[:, 1], packed[:, r], 4, None, ALU.arith_shift_right).then_inc(s_nib, 1)
                            wait(dve, s_nib, t + 1)
                            zero = zs[:, 0, one, :].rearrange("p a g -> p (a g)").unsqueeze(2).to_broadcast([P, NG, GROUP // 2])
                            scale = zs[:, 1, one, :].rearrange("p a g -> p (a g)").unsqueeze(2).to_broadcast([P, NG, GROUP])
                            tile = wf[:, one, :].rearrange("p b n -> p (b n)")
                            pairs = tile.rearrange("p (g m a) -> p a g m", g=NG, a=2)
                            for a in range(2):
                                ins = nc.vector.tensor_tensor(pairs[:, a], nib[:, a].rearrange("p (g m) -> p g m", g=NG), zero,
                                                              ALU.subtract)
                            ins.then_inc(s_fc, 1)
                            wait(dve, s_fc, 3 * t + 1)
                            grouped = tile.rearrange("p (g m) -> p g m", g=NG)
                            nc.vector.tensor_tensor(grouped, grouped, scale, ALU.mult).then_inc(s_fc, 1)
                            wait(dve, s_fc, 3 * t + 2)
                            nc.vector.tensor_reduce(fmx[:, one], tile, AX.X, ALU.max, apply_absolute_value=True).then_inc(s_fc, 1)

                        for m in range(CH):
                            rotate(m)
                            if m >= 1:
                                low(m - 1)
                            if m == 0:
                                split(g, 1)
                            if m == TC and not last:
                                split(g + 1, 0)
                            if m % TC == 2:
                                unpack(g, m // TC)
                        low(CH - 1)
                    split(0, 0)
                    group(0)
                    with dve.Fori(1, NGRP - 1) as g:
                        group(g)
                    group(NGRP - 1, last=True)

                    done = [3 * D // P]

                    def chain(ins):
                        done[0] += 1
                        ins.then_inc(s_fc, 1)
                        dve.wait_ge(s_fc, done[0])

                    dve.wait_ge(s_fc, done[0])
                    nc.vector.tensor_reduce(fmx[:, D // P:D // P + 1], fmx[:, 0:D // P], AX.X, ALU.max).then_inc(s_fm, 1)
                    dve.wait_ge(s_fa, 1)
                    pow2_scales(dve, chain, 4, 5)
                    chain(nc.vector.tensor_scalar(ffn_scale[:], w_down[:, 4:5], 1.0 / XN_SCALE, None, ALU.mult))

                @block.tensor
                def _(pe):
                    def group(g):
                        first = isinstance(g, int)
                        for w in range(2):
                            wait(pe, s_qwh, 4 * g + 2 * w + 2)
                            wait(pe, s_qwl, 2 * g + w + 1)
                            for tc in range(TC):
                                m = w * TC + tc
                                k = m % 2
                                n = g * CH + m
                                if m >= 2 or not first:
                                    wait(pe, s_pr, n - 1)
                                for ab in range(2):
                                    acc = banks[2 * k + ab]
                                    for c in range(IC):
                                        hi = xnT_h[:, c, 512 * tc:512 * tc + 512]
                                        lo = xnT_l[:, c, 512 * tc:512 * tc + 512]
                                        pe.matmul(acc[:], wh[:, w, c, ab], hi, start=(c == 0), stop=False)
                                        pe.matmul(acc[:], wh[:, w, c, ab], lo, start=False, stop=False)
                                        ins = pe.matmul(acc[:], wl[:, w, c, ab], hi, start=False, stop=(c == IC - 1))
                                ins.then_inc(s_ps, 1)
                    group(0)
                    with pe.Fori(1, NGRP) as g:
                        group(g)

        step3_to_5(nc, whole, unpacked, sb, sem, banks, ident, xnT_h, xnT_l, w_up,
                   exp_scale, attn_scale, ffn_scale, q_scr, k_scr, v_scr, y_scr, o_scr, x_tiles, out_tiles,
                   wo, wf, wfT_h, wfT_l)


def step3_to_5(nc, whole, unpacked, sb, sem, banks, ident, xnT_h, xnT_l, w_up,
               exp_scale, attn_scale, ffn_scale, q_scr, k_scr, v_scr, y_scr, o_scr, x_tiles, out_tiles,
               wo, wf, wfT_h, wfT_l):
    step3 = ExitStack()
    with step3:
        OT = D // P
        wf_h = sb(step3, "wf_h", [P, 2, D], F16)
        wf_l = sb(step3, "wf_l", [P, 2, D], F16)
        s_fh = sem("ffn_high_ready")
        s_fl = sem("ffn_low_ready")
        s_ft = sem("ffn_transposed")
        s_fth = sem("ffn_high_stored")
        s_ftl = sem("ffn_low_stored")
        with nc.Block("transpose_ffn") as block:
            @block.scalar
            def _(act):
                for t in range(OT):
                    wait(act, s_ft, 2 * (t - 1))
                    act.activation(wf_h[:, t % 2], wf[:, t], ACT.Copy, scale=w_up[:, 4:5]).then_inc(s_fh, 1)
                    act.wait_ge(s_ft, 2 * t + 1)
                    act.activation(wfT_h[:, :, t * P:(t + 1) * P],
                                   banks[2 * (t % 2)][:].bitcast(F16).rearrange("p (c s) -> p c s", s=P),
                                   ACT.Copy).then_inc(s_fth, 1)

            @block.vector
            def _(dve):
                for t in range(OT):
                    dve.wait_ge(s_fh, t + 1)
                    wait(dve, s_ft, 2 * (t - 1))
                    nc.vector.scalar_tensor_tensor(wf_l[:, t % 2], wf[:, t], w_up[:, 4:5], wf_h[:, t % 2],
                                                   ALU.mult, ALU.subtract).then_inc(s_fl, 1)
                    dve.wait_ge(s_ft, 2 * t + 2)
                    nc.vector.tensor_copy(wfT_l[:, :, t * P:(t + 1) * P],
                                          banks[1 + 2 * (t % 2)][:].bitcast(F16).rearrange("p (c s) -> p c s", s=P)
                                          ).then_inc(s_ftl, 1)

            @block.tensor
            def _(pe):
                for t in range(OT):
                    for part, ready, read, bank in ((wf_h, s_fh, s_fth, 0), (wf_l, s_fl, s_ftl, 1)):
                        pe.wait_ge(ready, t + 1)
                        wait(pe, read, t - 1)
                        dst = banks[bank + 2 * (t % 2)][:].bitcast(F16)
                        for c in range(IC):
                            ins = pe.transpose(dst[:, c * P:(c + 1) * P], part[:, t % 2, c * P:(c + 1) * P], ident[:])
                        ins.then_inc(s_ft, 1)

    unpacked.close()

    step4 = ExitStack()
    with step4:
        KR = 3 * HD
        q_st = sb(step4, "q_st", [P, 4, S], F16)
        k_st = sb(step4, "k_st", [P, 4, S], F16)
        v_st = sb(step4, "v_in", [P, 4, 2, 4 * VW], F16)
        p32 = sb(step4, "p32", [P, UNITS * 512], F32)
        p_h = sb(step4, "p_h", [P, 2, UNITS * 512], F16)
        p_l = sb(step4, "p_l", [P, 2, UNITS * 512], F16)
        neg_id = sb(step4, "neg_id", [P, P], mybir.dt.bfloat16)
        past = sb(step4, "past", [P, 2, P], mybir.dt.bfloat16)
        mx = sb(step4, "mx", [P, 2, QT], F32)
        row_max = sb(step4, "row_max", [P, QT], F32)
        m_row = sb(step4, "m_row", [P, 2 * QT], F16)
        mT = sb(step4, "mT", [2 * QT, 2, P], F16)
        c32 = sb(step4, "c32", [P, 2, QT, VW], F32)
        rsum = sb(step4, "rsum", [P, QT], F32)
        osum = sb(step4, "osum", [P, QT, HD], F32)
        o32 = sb(step4, "o32", [P, QT, 4, HD], F32)
        o_h = sb(step4, "o_h", [P, QT * P], F16)
        o_l = sb(step4, "o_l", [P, QT * P], F16)
        oT_s = sb(step4, "oT_s", [P, 2, QT * P], F16)
        xf = sb(step4, "xf", [P, D], F32)
        y_st = sb(step4, "y_st", [P, D], F32)
        ACT_HIGH = 7 * 512
        POOL_W = 9 * P
        a_bank = [banks[0], banks[1], banks[5]]
        b_bank = [banks[2], banks[3], banks[7]]
        turn_bank, ffn_bank = banks[4], banks[6]

        s_ld = [sem(f"qk_loaded{k}") for k in range(4)]
        s_ldv = [sem(f"v_loaded{k}") for k in range(4)]
        s_const = sem("constants_ready")
        s_mrow = [sem(f"max_rows_loaded{k}") for k in range(4)]
        s_a = sem("score_segment_ready")
        s_max = sem("segment_max_ready")
        s_mc = sem("max_small_done")
        s_mr = sem("max_columns_ready")
        s_mt = sem("max_transposed")
        s_mcp = sem("max_rows_ready")
        s_b = sem("scoresT_unit_ready")
        s_exp = sem("probs_unit_ready")
        s_hi = sem("probs_high_act_ready")
        s_hid = sem("probs_high_dve_ready")
        s_lo = sem("probs_low_dve_ready")
        s_lop = sem("probs_low_pool_ready")
        s_pv = sem("pv_tile_ready")
        s_c = sem("pv_half_copied")
        s_nc = sem("norm_small_done")
        s_norm = sem("head_normalised")
        s_oh = sem("o_high_ready")
        s_ol = sem("o_low_ready")
        s_ot = sem("o_transposed")
        s_oth = sem("oT_high_stored")
        s_otl = sem("oT_low_stored")
        s_ow = sem("oT_written")
        s_f = sem("ffn_half_ready")
        s_fe = sem("ffn_half_added")
        s_xf = [sem(f"x_half_loaded{k}") for k in range(2)]
        s_yw = [sem(f"y_half_written{k}") for k in range(2)]
        GROUPS = PAIRS // 4

        def rounds(eng, body):
            body(0, True, False)
            with eng.Fori(1, GROUPS - 1) as i:
                body(i, False, False)
            body(GROUPS - 1, False, True)

        with nc.Block("attention") as block:
            @block.sync
            def _(sp):
                def load_qk(i, j):
                    k = j % 4
                    n = held(sp, 4 * i + j)
                    if not (isinstance(i, int) and n < 4):
                        wait(sp, s_b, UNITS * (n - 3))
                    q_all = q_scr.rearrange("b h r d s -> (b h) (r d) s")[bass.ds(n, 1)].rearrange("a r s -> (a r) s")
                    k_all = k_scr.rearrange("b h r d s -> (b h) (r d) s")[bass.ds(n, 1)].rearrange("a r s -> (a r) s")
                    sp.dma_start(q_st[0:2 * HD, k], q_all).then_inc(s_ld[k], 16)
                    sp.dma_start(q_st[2 * HD:KR, k], q_all[0:HD]).then_inc(s_ld[k], 16)
                    sp.dma_start(k_st[0:HD, k], k_all[0:HD]).then_inc(s_ld[k], 16)
                    sp.dma_start(k_st[HD:KR, k], k_all).then_inc(s_ld[k], 16)

                def load_v(i, j):
                    k = j % 4
                    n = held(sp, 4 * i + j)
                    if not (isinstance(i, int) and n < 4):
                        wait(sp, s_pv, QT * (n - 3))
                    v_all = v_scr.rearrange("b h t p c -> (b h) t p c")[bass.ds(n, 1)].rearrange("a t p c -> p (a t) c")
                    sp.dma_start(v_st[:, k], v_all).then_inc(s_ldv[k], 16)

                def max_rows(i, j):
                    n = 4 * i + j
                    wait(sp, s_mcp, n + 1)
                    for r in range(2):
                        sp.dma_start(q_st[KR + r:KR + r + 1, j % 4, :].rearrange("a (t s) -> a t s", s=P),
                                     mT[r * QT:(r + 1) * QT, j % 2, :]).then_inc(s_mrow[j % 4], 16)

                def ffn_half(i, hf):
                    cs = slice(512 * hf, 512 * hf + 512)
                    last = i if hf == 0 else held(sp, i - 1)
                    nxt = held(sp, last + 1)
                    store = not (isinstance(last, int) and last < 0)
                    load = not (isinstance(nxt, int) and nxt >= GROUPS)
                    if store:
                        wait(sp, s_fe, 2 * last + hf + 1)
                    for what in (("load", "store") if hf == 0 else ("store", "load")):
                        if what == "store" and store:
                            sp.dma_start(y_scr[bass.ds(last, 1), :, cs].rearrange("a p c -> (a p) c"),
                                         y_st[:, cs]).then_inc(s_yw[hf], 16)
                        if what == "load" and load:
                            sp.dma_start(xf[:, cs], x_tiles[bass.ds(nxt, 1), :, cs].rearrange("a p c -> (a p) c")
                                         ).then_inc(s_xf[hf], 16)

                for j in range(3):
                    load_qk(0, j)
                for j in range(3):
                    load_v(0, j)
                sp.dma_start(xf[:, 0:512], x_tiles[0, :, 0:512]).then_inc(s_xf[0], 16)
                max_rows(0, 0)

                def body(i, first, last):
                    for j in range(4):
                        if j == 0:
                            ffn_half(i, 1)
                        if j == 2:
                            ffn_half(i, 0)
                        if not (last and j >= 1):
                            load_qk(i, j + 3)
                        if not (last and j == 3):
                            max_rows(i, j + 1)
                        if not (last and j >= 1):
                            load_v(i, j + 3)
                        if j == 3 and not first:
                            store_group(i - 1)

                def store_group(g):
                    g = held(sp, g)
                    count = held(sp, g + 1)
                    wait(sp, s_oth, count)
                    wait(sp, s_otl, count)
                    sp.dma_start(o_scr[bass.ds(g, 1)].rearrange("a p r s -> (a p) r s"), oT_s[:]).then_inc(s_ow, 16)

                rounds(sp, body)
                ffn_half(GROUPS, 1)
                store_group(GROUPS - 1)
                sp.wait_ge(s_ow, 16 * (GROUPS + 1))
                for hf in range(2):
                    sp.wait_ge(s_yw[hf], 16 * GROUPS)

            @block.gpsimd
            def _(pool):
                pool.memset(neg_id[:], 0.0).then_inc(s_const, 1)
                pool.memset(past[:], MASKED).then_inc(s_const, 1)
                pool.memset(mx[:, 1, 0:4], -3.0e38).then_inc(s_const, 1)
                pool.wait_ge(s_const, 3)
                pool.affine_select(out=neg_id[:], in_=neg_id[:], compare_op=ALU.not_equal, fill=-MASKED,
                                   base=0, pattern=[[-1, P]], channel_multiplier=1).then_inc(s_const, 1)
                for side in range(2):
                    sign = 1 - 2 * side
                    pool.affine_select(out=past[:, side], in_=past[:, side], compare_op=ALU.is_gt, fill=0.0, base=0,
                                       pattern=[[sign, P]], channel_multiplier=-sign).then_inc(s_const, 1)
                pool.wait_ge(s_const, 6)
                pool.memset(k_st[KR:KR + 2, :, :], 1.0 / MAX_SCALE).then_inc(s_const, 1)
                pool.memset(oT_s[0:1, 0, 0:1], 0.0).then_inc(s_ow, 16)

                def group_low(i):
                    wait(pool, s_oh, i)
                    nc.gpsimd.tensor_tensor(o_l[:], o32[:].rearrange("p t h d -> p (t h d)"), o_h[:],
                                            ALU.subtract).then_inc(s_ol, 1)

                def body(i, first, last):
                    for j in range(4):
                        n = 4 * i + j
                        for c in range(CHUNKS):
                            if c == 2 and j == 1 and not first:
                                group_low(i)
                            cs = slice((c + 1) * CW - POOL_W, (c + 1) * CW)
                            wait(pool, s_hi, CHUNKS * n + c + 1)
                            if c == 2:
                                wait(pool, s_hid, n + 1)
                            nc.gpsimd.tensor_tensor(p_l[:, j % 2, cs], p32[:, cs], p_h[:, j % 2, cs],
                                                    ALU.subtract).then_inc(s_lop, 1)
                rounds(pool, body)
                group_low(GROUPS)

            @block.scalar
            def _(act):
                def copy_rows(i, j):
                    n = 4 * i + j
                    wait(act, s_mt, n + 1)
                    if not (isinstance(i, int) and n < 2):
                        wait(act, s_mrow[(j - 2) % 4], 32 * (i + (j - 2) // 4 + 1))
                    act.activation(mT[:, j % 2, :], turn_bank[0:2 * QT].bitcast(F16)[:, 0:P], ACT.Copy).then_inc(s_mcp, 1)

                def copy_pv(i, j, half):
                    n = 4 * i + j
                    wait(act, s_pv, QT * n + 4 * (half + 1))
                    if half == 0:
                        wait(act, s_norm, n - 1)
                    act.activation(c32[:, j % 2, 4 * half:4 * half + 4, :].rearrange("p t c -> p (t c)"),
                                   turn_bank[:, 0:4 * VW], ACT.Copy).then_inc(s_c, 1)

                def group_high(i):
                    wait(act, s_norm, 4 * i)
                    act.activation(o_h[:], o32[:].rearrange("p t h d -> p (t h d)"), ACT.Copy).then_inc(s_oh, 1)

                def group_out(i, part):
                    wait(act, s_ot, 2 * (i - 1) + part + 1)
                    if part == 0:
                        wait(act, s_ow, 16 * i)
                    act.activation(oT_s[:, part], turn_bank[:].bitcast(F16), ACT.Copy).then_inc((s_oth, s_otl)[part], 1)

                copy_rows(0, 0)

                def body(i, first, last):
                    for j in range(4):
                        n = 4 * i + j

                        def exps(u):
                            c = u // CHUNK
                            wait(act, s_b, UNITS * n + u + 1)
                            if u % CHUNK == 0:
                                wait(act, s_hi, CHUNKS * (n - 1) + c + 1)
                                if c == 2:
                                    wait(act, s_hid, n)
                                wait(act, s_lo, CHUNKS * (n - 1) + c + 1)
                                wait(act, s_lop, CHUNKS * (n - 1) + c + 1)
                            act.activation(p32[:, 512 * u:512 * u + 512], b_bank[u % 3][:], ACT.Exp,
                                           scale=exp_scale[:]).then_inc(s_exp, 1)

                        def high(c):
                            end = min((c + 1) * CW, ACT_HIGH)
                            wait(act, s_exp, UNITS * n + end // 512)
                            if c == 0:
                                wait(act, s_pv, QT * (n - 1))
                            act.activation(p_h[:, j % 2, c * CW:end], p32[:, c * CW:end],
                                           ACT.Copy).then_inc(s_hi, 1)

                        exps(0)
                        if not (first and j <= 1):
                            copy_pv(i, j - 2, 1)
                        exps(1)
                        exps(2)
                        if not (last and j == 3):
                            copy_rows(i, j + 1)
                        exps(3)
                        high(0)
                        if j in (2, 3) and not first:
                            group_out(i, j - 2)
                        exps(4)
                        exps(5)
                        if not (first and j == 0):
                            copy_pv(i, j - 1, 0)
                        exps(6)
                        high(1)
                        if j == 1 and not first:
                            group_high(i)
                        exps(7)
                        exps(8)
                        high(2)
                rounds(act, body)
                copy_pv(GROUPS - 1, 2, 1)
                copy_pv(GROUPS - 1, 3, 0)
                copy_pv(GROUPS - 1, 3, 1)
                group_high(GROUPS)
                group_out(GROUPS, 0)
                group_out(GROUPS, 1)

            @block.vector
            def _(dve):
                dve.wait_ge(s_const, 7)

                def seg_max(i, j, s):
                    n = 4 * i + j
                    t, k0, w, diagonal = SEGMENTS[s]
                    wait(dve, s_a, NSEG * n + s + 1)
                    src = a_bank[s % 3][:, 0:w]
                    nc.vector.tensor_reduce(mx[:, k0 // 512, t:t + 1], src, AX.X, ALU.max).then_inc(s_max, 1)

                def row_maxima(i, j):
                    n = 4 * i + j
                    wait(dve, s_max, NSEG * (n + 1))
                    nc.vector.tensor_tensor(row_max[:], mx[:, 0], mx[:, 1], ALU.max).then_inc(s_mc, 1)

                def max_high(i, j):
                    n = 4 * i + j
                    wait(dve, s_mc, 2 * n + 1)
                    wait(dve, s_mt, n)
                    nc.vector.tensor_scalar(m_row[:, 0:QT], row_max[:], -MAX_SCALE, None, ALU.mult).then_inc(s_mc, 1)

                def max_low(i, j):
                    n = 4 * i + j
                    wait(dve, s_mc, 2 * n + 2)
                    nc.vector.scalar_tensor_tensor(m_row[:, QT:2 * QT], row_max[:], -MAX_SCALE, m_row[:, 0:QT],
                                                   ALU.mult, ALU.subtract).then_inc(s_mr, 1)

                def high(i, j):
                    n = 4 * i + j
                    wait(dve, s_exp, UNITS * (n + 1))
                    nc.vector.tensor_copy(p_h[:, j % 2, ACT_HIGH:], p32[:, ACT_HIGH:]).then_inc(s_hid, 1)

                def low(i, j, c):
                    n = 4 * i + j
                    cs = slice(c * CW, (c + 1) * CW - POOL_W)
                    wait(dve, s_hi, CHUNKS * n + c + 1)
                    nc.vector.tensor_tensor(p_l[:, j % 2, cs], p32[:, cs], p_h[:, j % 2, cs], ALU.subtract).then_inc(s_lo, 1)

                def sum_parts(i, j):
                    wait(dve, s_c, 2 * (4 * i + j) + 2)
                    wait(dve, s_norm, 4 * i + j)
                    sums = c32[:, j % 2]
                    nc.vector.reciprocal(rsum[:], sums[:, :, 2 * HD])
                    nc.vector.tensor_tensor(osum[:], sums[:, :, 0:HD], sums[:, :, HD:2 * HD], ALU.add).then_inc(s_nc, 1)

                def normalise(i, j):
                    if j % 4 == 0:
                        wait(dve, s_ol, i + j // 4)
                    wait(dve, s_nc, 4 * i + j + 1)
                    nc.vector.tensor_tensor(o32[:, :, j % 4, :], osum[:], rsum[:].unsqueeze(2).to_broadcast([P, QT, HD]),
                                            ALU.mult).then_inc(s_norm, 1)

                def ffn_add(i, hf):
                    cs = slice(512 * hf, 512 * hf + 512)
                    wait(dve, s_f, 2 * i + hf + 1)
                    wait(dve, s_xf[hf], 16 * (i + 1))
                    wait(dve, s_yw[hf], 16 * i)
                    nc.vector.scalar_tensor_tensor(y_st[:, cs], ffn_bank[:], ffn_scale[:], xf[:, cs],
                                                   ALU.mult, ALU.add).then_inc(s_fe, 1)

                for j in range(2):
                    for s in range(NSEG):
                        seg_max(0, j, s)
                    row_maxima(0, j)
                    if j == 0:
                        max_high(0, j)
                        max_low(0, j)

                def body(i, first, last):
                    for j in range(4):
                        ahead = not (last and j >= 2)
                        behind = not (first and j == 0)

                        def maxima(s0, s1):
                            if ahead:
                                for s in range(s0, s1):
                                    seg_max(i, j + 2, s)

                        if not (last and j == 3):
                            max_high(i, j + 1)
                        maxima(0, 1)
                        if not (last and j == 3):
                            max_low(i, j + 1)
                        maxima(1, 3)
                        if behind:
                            high(i, j - 1)
                        behind2 = not (first and j <= 1)
                        maxima(3, 4)
                        if behind:
                            low(i, j - 1, 2)
                        maxima(4, 5)
                        if j == 1 and behind2:
                            sum_parts(i, j - 2)
                        maxima(5, 6)
                        if j == 1 and behind2:
                            normalise(i, j - 2)
                        maxima(6, 7)
                        low(i, j, 0)
                        maxima(7, 10)
                        if j != 1 and behind2:
                            sum_parts(i, j - 2)
                        maxima(10, 11)
                        if j != 1 and behind2:
                            normalise(i, j - 2)
                        if j % 2 == 1:
                            ffn_add(i, j // 2)
                        maxima(11, NSEG)
                        if ahead:
                            row_maxima(i, j + 2)
                        low(i, j, 1)
                rounds(dve, body)
                high(GROUPS - 1, 3)
                low(GROUPS - 1, 3, 2)
                for j in (2, 3):
                    sum_parts(GROUPS - 1, j)
                    normalise(GROUPS - 1, j)

            @block.tensor
            def _(pe):
                pe.wait_ge(s_const, 7)

                def segment(i, j, s):
                    n, k = 4 * i + j, j % 4
                    t, k0, w, diagonal = SEGMENTS[s]
                    if s == 0:
                        wait(pe, s_ld[k], 64 * (i + j // 4 + 1))
                    wait(pe, s_max, NSEG * n + s - 2)
                    ins = pe.matmul(a_bank[s % 3][:, 0:w], q_st[0:KR, k, t * P:(t + 1) * P], k_st[0:KR, k, k0:k0 + w],
                                    start=True, stop=not diagonal)
                    if diagonal:
                        ins = pe.matmul(a_bank[s % 3][:, w - P:w], neg_id[:], past[:, 0], start=False, stop=True)
                    ins.then_inc(s_a, 1)

                def unit(i, j, u):
                    n, k = 4 * i + j, j % 4
                    if u == 0:
                        wait(pe, s_mrow[k], 32 * (i + 1))
                    wait(pe, s_exp, UNITS * n + u - 2)
                    acc = b_bank[u % 3]
                    for col, kt, t, tiles in unit_runs(u):
                        diagonal = t == kt
                        ins = pe.matmul(acc[:, col:col + tiles * P], k_st[0:KR + 2, k, kt * P:(kt + 1) * P],
                                        q_st[0:KR + 2, k, t * P:(t + tiles) * P], start=True, stop=not diagonal)
                        if diagonal:
                            ins = pe.matmul(acc[:, col:col + P], neg_id[:], past[:, 1], start=False, stop=True)
                    ins.then_inc(s_b, 1)

                def pv(i, j, t, turn_before):
                    n, k = 4 * i + j, j % 4
                    if t in (0, 3):
                        chunks = CHUNKS * n + (2 if t == 0 else 3)
                        wait(pe, s_hi, chunks)
                        if t == 3:
                            wait(pe, s_hid, n + 1)
                        wait(pe, s_lo, chunks)
                        wait(pe, s_lop, chunks)
                    if t == 0:
                        wait(pe, *turn_before)
                        wait(pe, s_ldv[k], 16 * (i + j // 4 + 1))
                    if t == 4:
                        wait(pe, s_c, 2 * n + 1)
                    acc = turn_bank[:, (t % 4) * VW:(t % 4 + 1) * VW]
                    for kt in range(t + 1):
                        at = SLOT[(kt, t)] * P
                        v = v_st[:, k, kt // 4, (kt % 4) * VW:(kt % 4 + 1) * VW]
                        pe.matmul(acc, p_h[:, j % 2, at:at + P], v, start=(kt == 0), stop=False)
                        ins = pe.matmul(acc, p_l[:, j % 2, at:at + P], v, start=False, stop=(kt == t))
                    ins.then_inc(s_pv, 1)

                def transpose_max(i, j, turn_before=None):
                    wait(pe, s_mr, 4 * i + j + 1)
                    if turn_before is not None:
                        wait(pe, *turn_before)
                    pe.transpose(turn_bank[0:2 * QT].bitcast(F16)[:, 0:P], m_row[:], ident[:]).then_inc(s_mt, 1)

                def transpose_group(i, part, turn_sem, turn):
                    src = (o_h, o_l)[part]
                    wait(pe, (s_oh, s_ol)[part], i)
                    wait(pe, turn_sem, turn)
                    for t in range(QT):
                        ins = pe.transpose(turn_bank[:].bitcast(F16)[:, t * P:(t + 1) * P], src[:, t * P:(t + 1) * P], ident[:])
                    ins.then_inc(s_ot, 1)

                def ffn(i, j):
                    hf = j // 2
                    if j % 2 == 0:
                        wait(pe, s_fe, 2 * i + hf)
                    for c in range(4 * (j % 2), 4 * (j % 2) + 4):
                        at = bass.ds(i * P, P)
                        cs = slice(512 * hf, 512 * hf + 512)
                        pe.matmul(ffn_bank[:], xnT_h[:, c, at], wfT_h[:, c, cs], start=(c == 0), stop=False)
                        pe.matmul(ffn_bank[:], xnT_h[:, c, at], wfT_l[:, c, cs], start=False, stop=False)
                        ins = pe.matmul(ffn_bank[:], xnT_l[:, c, at], wfT_h[:, c, cs], start=False, stop=(c == IC - 1))
                        yield
                    if j % 2 == 1:
                        ins.then_inc(s_f, 1)
                    yield

                for j in range(2):
                    for s in range(NSEG):
                        segment(0, j, s)
                    if j == 0:
                        transpose_max(0, 0)

                def body(i, first, last):
                    for j in range(4):
                        n = 4 * i + j
                        ahead = not (last and j >= 2)
                        behind = not (first and j == 0)
                        turn = (s_mcp, n + 1) if first and j <= 1 else (s_c, 2 * (n - 1))
                        filler = ffn(i, j)
                        for u in range(UNITS):
                            unit(i, j, u)
                            if ahead:
                                for s in SEGMENTS_AFTER_UNIT[u]:
                                    segment(i, j + 2, s)
                            if u % 2 == 1:
                                next(filler)
                            if u == 2 and not (last and j == 3):
                                transpose_max(i, j + 1, turn)
                                turn = (s_mcp, n + 2)
                            if u == 4 and j in (2, 3) and not first:
                                transpose_group(i, j - 2, *turn)
                                turn = ((s_oth, s_otl)[j - 2], i)
                            if behind:
                                for t in {5: (0, 1, 2, 3), 7: (4, 5), 8: (6, 7)}.get(u, ()):
                                    pv(i, j - 1, t, turn)
                        next(filler)
                rounds(pe, body)
                for t in range(QT):
                    pv(GROUPS - 1, 3, t, (s_c, 2 * (PAIRS - 1)))
                transpose_group(GROUPS, 0, s_c, 2 * PAIRS)
                transpose_group(GROUPS, 1, s_oth, GROUPS)

    step5 = ExitStack()
    with step5:
        wo_raw = sb(step5, "wo_raw", [P, IC, D], F32)
        wo_h = sb(step5, "wo_h", [P, IC, D], F16)
        wo_l = sb(step5, "wo_l", [P, IC, D], F16)
        y_in = sb(step5, "y_in", [P, 2, D], F32)
        y_out = sb(step5, "y_out", [P, 2, D], F32)
        oT = (xnT_h, xnT_l)
        s_wo = [sem(f"wo_loaded{c}") for c in range(4)]
        s_oT = [sem(f"oT_loaded{c}") for c in range(4)]
        s_woh = sem("wo_high_ready")
        s_wol = sem("wo_low_ready")
        s_y = [sem(f"y_loaded{k}") for k in range(2)]
        s_op = sem("out_product_ready")
        s_add = sem("out_added")
        s_out = [sem(f"out_written{k}") for k in range(2)]
        with nc.Block("project") as block:
            @block.sync
            def _(sp):
                view = wo.rearrange("(c p) n -> p c n", p=P)

                def load_o(c):
                    for r in range(2):
                        src = o_scr[IC * (c // 2):IC * (c // 2 + 1), :, r, 512 * (c % 2):512 * (c % 2) + 512]
                        sp.dma_start(oT[r][:, :, 512 * c:512 * c + 512], src.rearrange("c p s -> p c s")).then_inc(s_oT[c], 16)

                for c in range(4):
                    sp.dma_start(wo_raw[:, 2 * c:2 * c + 2, :], view[:, 2 * c:2 * c + 2, :]).then_inc(s_wo[c], 16)
                    if c == 0:
                        load_o(0)
                for k in range(2):
                    sp.dma_start(y_in[:, k], y_scr[k]).then_inc(s_y[k], 16)
                for c in range(1, 4):
                    load_o(c)

                def body(i, last):
                    for k in range(2):
                        t = held(sp, 2 * i + k)
                        ahead = held(sp, t + 2)
                        wait(sp, s_add, 2 * t + 2)
                        sp.dma_start(out_tiles[bass.ds(t, 1)].rearrange("a p d -> (a p) d"), y_out[:, k]).then_inc(s_out[k], 16)
                        if not last:
                            sp.dma_start(y_in[:, k], y_scr[bass.ds(ahead, 1)].rearrange("a p d -> (a p) d")).then_inc(s_y[k], 16)
                with sp.Fori(0, TT // 2 - 1) as i:
                    body(i, False)
                body(TT // 2 - 1, True)
                for k in range(2):
                    sp.wait_ge(s_out[k], 16 * TT // 2)

            @block.scalar
            def _(act):
                for c in range(IC):
                    act.wait_ge(s_wo[c // 2], 16)
                    act.activation(wo_h[:, c, :], wo_raw[:, c, :], ACT.Copy, scale=w_up[:, 3:4]).then_inc(s_woh, 1)

            @block.vector
            def _(dve):
                for c in range(IC):
                    dve.wait_ge(s_woh, c + 1)
                    nc.vector.scalar_tensor_tensor(wo_l[:, c, :], wo_raw[:, c, :], w_up[:, 3:4], wo_h[:, c, :],
                                                   ALU.mult, ALU.subtract).then_inc(s_wol, 1)

                def body(i, first):
                    for k in range(2):
                        t = 2 * i + k
                        for n in range(2):
                            cs = slice(512 * n, 512 * n + 512)
                            wait(dve, s_op, 2 * t + n + 1)
                            if n == 0:
                                wait(dve, s_y[k], 16 * (i + 1))
                                if not first:
                                    wait(dve, s_out[k], 16 * i)
                            nc.vector.scalar_tensor_tensor(y_out[:, k, cs], banks[2 * k + n][:], attn_scale[:],
                                                           y_in[:, k, cs], ALU.mult, ALU.add).then_inc(s_add, 1)
                body(0, True)
                with dve.Fori(1, TT // 2) as i:
                    body(i, False)

            @block.tensor
            def _(pe):

                def products(acc, t, n, c):
                    cs = slice(512 * n, 512 * n + 512)
                    at = bass.ds(t * P, P)
                    pe.matmul(acc[:], oT[0][:, c, at], wo_h[:, c, cs], start=(c == 0), stop=False)
                    pe.matmul(acc[:], oT[0][:, c, at], wo_l[:, c, cs], start=False, stop=False)
                    return pe.matmul(acc[:], oT[1][:, c, at], wo_h[:, c, cs], start=False, stop=(c == IC - 1))

                pe.wait_ge(s_oT[0], 32)
                for c in range(IC):
                    pe.wait_ge(s_woh, c + 1)
                    pe.wait_ge(s_wol, c + 1)
                    for t in range(2):
                        for n in range(2):
                            ins = products(banks[2 * t + n], t, n, c)
                            if c == IC - 1:
                                ins.then_inc(s_op, 1)
                for c in range(1, 4):
                    pe.wait_ge(s_oT[c], 32)
                with pe.Fori(1, TT // 2) as i:
                    for k in range(2):
                        t = 2 * i + k
                        for n in range(2):
                            wait(pe, s_add, 2 * (t - 2) + n + 1)
                            for c in range(IC):
                                ins = products(banks[2 * k + n], t, n, c)
                            ins.then_inc(s_op, 1)


_INS = ["L0_attn_x", "L0_attn_wq", "L0_attn_wk", "L0_attn_wv", "L0_attn_wo", "L0_ffn_W_q", "L0_ffn_scale", "L0_ffn_zero"]


def kernel(**inputs):
    import numpy as _np
    import concourse.bacc as _bacc
    from concourse import mybir as _mybir
    from concourse.bass_utils import run_bass_kernel_spmd as _run

    nc = _bacc.Bacc("TRN2", target_bir_lowering=False, num_devices=1)
    arrays, args = {}, []

    def give(name, a):
        a = _np.ascontiguousarray(a)
        arrays[name] = a
        args.append(nc.dram_tensor(name, a.shape, _mybir.dt.from_np(a.dtype), kind="ExternalInput").ap())

    for name in _INS:
        give(f"in_{name}", inputs[name])
    inv = 1.0 / 10000.0 ** (_np.arange(0, HD, 2)[:HD // 2].astype(_np.float32) / HD)
    angle = _np.outer(_np.arange(S), inv).astype(_np.float32)
    for name, f in (("cos_table", _np.cos), ("sin_table", _np.sin)):
        give(name, _np.tile(f(angle).T * _np.float32(QK_SCALE), (P // (HD // 2), 1)).astype(_np.float32))
    args.append(nc.dram_tensor("out_0_dram", (B, S, D), F32, kind="ExternalOutput").ap())
    build(nc, *args)
    r = _run(nc, [arrays], core_ids=[0])
    return r.results[0]["out_0_dram"]
```
